# Optimizing a Trainium2 kernel written in Bass

```python
import numpy as np
import jax
import jax.numpy as jnp

def _softmax(x, axis=-1):
    return jax.nn.softmax(x, axis=axis)

def _gelu(x):
    return jax.nn.gelu(x, approximate=True)

def _silu(x):
    return jax.nn.silu(x)

def _sigmoid(x):
    return jax.nn.sigmoid(x)

def _layernorm(x, axis=-1, eps=1e-05):
    m = jnp.mean(x, axis=axis, keepdims=True)
    v = jnp.var(x, axis=axis, keepdims=True)
    return (x - m) / jnp.sqrt(v + eps)

def _scatter_add(tgt, idx, src, axis=0):
    return tgt.at[idx].add(src)

def _segment_sum(src, seg, n):
    return jax.ops.segment_sum(src, seg, n)
kernel_name = 'mk_gnn_resnorm_d2_gnn_r64_40e1db'

def setup_inputs(seed: int=0):
    np.random.seed(seed)
    _w = jnp.asarray

    def _rec_inputs():
        import jax
        import jax.numpy as jnp
        _gk = jax.random.key(seed)
        x = -0.0009044 + 1 * jax.random.normal(jax.random.fold_in(_gk, 1), (100000, 32), jnp.float32)
        src = jax.random.randint(jax.random.fold_in(_gk, 2), (25000,), 0, 100000, jnp.int32)
        dst = jnp.minimum((100000 * jax.random.uniform(jax.random.fold_in(_gk, 3), (25000,)) ** 2.0).astype(jnp.int32), 99999)
        _o = jnp.argsort(dst, stable=True)
        src = src[_o]
        dst = dst[_o]
        edge_attr_3 = 0.000844983 + 0.999762 * jax.random.normal(jax.random.fold_in(_gk, 11), (25000, 3), jnp.float32)
        edge_weight = jax.random.uniform(jax.random.fold_in(_gk, 13), (25000,), jnp.float32, 0.0, 1)
        edge_weight1 = jax.random.uniform(jax.random.fold_in(_gk, 14), (25000, 1), jnp.float32, 0.0, 1)
        return (x, src, dst, edge_attr_3, edge_weight, edge_weight1)
    x, src, dst, edge_attr_3, edge_weight, edge_weight1 = _rec_inputs()

    def _L0_gnn_setup():
        import jax, jax.numpy as jnp
        import numpy as np
        N = 50000
        E = 25000
        D = 32
        H = 32
        key = jax.random.key(seed)
        ks = jax.random.split(key, 12)
        inputs = jax.random.normal(ks[0], (N, D), dtype=jnp.float32)
        e = jax.random.uniform(ks[1], (E, 1), dtype=jnp.float32)
        edge_index = jax.random.randint(ks[2], (2, E), 0, N, dtype=jnp.int64)
        s = 0.05
        W1 = jax.random.normal(ks[3], (3 * D, H), dtype=jnp.float32) * s
        b1 = jnp.zeros((H,), dtype=jnp.float32)
        W2 = jax.random.normal(ks[4], (H, H), dtype=jnp.float32) * s
        b2 = jnp.zeros((H,), dtype=jnp.float32)
        W3 = jax.random.normal(ks[5], (H, H), dtype=jnp.float32) * s
        b3 = jnp.zeros((H,), dtype=jnp.float32)
        W4 = jax.random.normal(ks[6], (H, H), dtype=jnp.float32) * s
        b4 = jnp.zeros((H,), dtype=jnp.float32)
        return {'inputs': inputs, 'e': e, 'edge_index': edge_index, 'W1': W1, 'b1': b1, 'W2': W2, 'b2': b2, 'W3': W3, 'b3': b3, 'W4': W4, 'b4': b4}
    _L0_gnn_all = _L0_gnn_setup()
    _L0_gnn_in = {k: v for k, v in _L0_gnn_all.items() if k in ('W1', 'b1', 'W2', 'b2', 'W3', 'b3', 'W4', 'b4')}
    del _L0_gnn_all

    def _L1_gnn_setup():
        import jax, jax.numpy as jnp
        import numpy as np
        from math import factorial, pi, sqrt
        MUL = 8
        RS = [(MUL, 0), (MUL, 1)]
        N_NODES = 20000
        N_EDGES = 10000
        FEAT_DIM = sum((m * (2 * l + 1) for m, l in RS))
        R_DIM = sum((mo * mi * (2 * min(lo, li) + 1) for mo, lo in RS for mi, li in RS))
        HIDDEN = 64

        def _cg(j1, j2, j3, m1, m2, m3):
            if m1 + m2 != m3:
                return 0.0
            f = factorial
            pre = sqrt((2 * j3 + 1) * f(j3 + j1 - j2) * f(j3 - j1 + j2) * f(j1 + j2 - j3) / f(j1 + j2 + j3 + 1))
            pre *= sqrt(f(j3 + m3) * f(j3 - m3) * f(j1 - m1) * f(j1 + m1) * f(j2 - m2) * f(j2 + m2))
            kmin = max(0, j2 - j3 - m1, j1 - j3 + m2)
            kmax = min(j1 + j2 - j3, j1 - m1, j2 + m2)
            s = 0.0
            for k in range(kmin, kmax + 1):
                s += (-1) ** k / (f(k) * f(j1 + j2 - j3 - k) * f(j1 - m1 - k) * f(j2 + m2 - k) * f(j3 - j2 + m1 + k) * f(j3 - j1 - m2 + k))
            return pre * s

        def _w3j_complex(l1, l2, l3):
            w = np.zeros((2 * l1 + 1, 2 * l2 + 1, 2 * l3 + 1))
            for m1 in range(-l1, l1 + 1):
                for m2 in range(-l2, l2 + 1):
                    m3 = -(m1 + m2)
                    if abs(m3) <= l3:
                        w[m1 + l1, m2 + l2, m3 + l3] = (-1) ** (l1 - l2 - m3) / sqrt(2 * l3 + 1) * _cg(l1, l2, l3, m1, m2, -m3)
            return w

        def _A(l):
            A = np.zeros((2 * l + 1, 2 * l + 1), dtype=complex)
            A[l, l] = 1.0
            for m in range(1, l + 1):
                A[l + m, l + m] = (-1) ** m / sqrt(2)
                A[l + m, l - m] = 1.0 / sqrt(2)
                A[l - m, l - m] = 1j / sqrt(2)
                A[l - m, l + m] = -1j * (-1) ** m / sqrt(2)
            return A

        def real_w3j(l1, l2, l3):
            wc = _w3j_complex(l1, l2, l3).astype(complex)
            wr = np.einsum('abc,ma,nb,oc->mno', wc, _A(l1).conj(), _A(l2).conj(), _A(l3).conj())
            i = int(np.argmax(np.abs(wr)))
            ph = wr.flat[i] / abs(wr.flat[i])
            wr = wr / ph
            assert np.abs(wr.imag).max() < 1e-10
            return np.real(wr).astype(np.float32)
        _W3J = {}
        for _mo, _lo in RS:
            for _mi, _li in RS:
                for _lf in range(abs(_lo - _li), _lo + _li + 1):
                    if (_lo, _lf, _li) not in _W3J:
                        _W3J[_lo, _lf, _li] = jnp.asarray(real_w3j(_lo, _lf, _li))
        _NORM = []
        for _mo, _lo in RS:
            _num = sum((mi * (2 * min(_lo, li) + 1) for mi, li in RS))
            _NORM.append(sqrt(4.0 * pi) * sqrt(2.0 * _lo + 1.0) / sqrt(_num))
        _F_OFFS = [0] + list(np.cumsum([mi * (2 * li + 1) for mi, li in RS]))

        def spherical_harmonics(rel_vec):
            r = rel_vec / jnp.linalg.norm(rel_vec, axis=-1, keepdims=True)
            x, y, z = (r[:, 0], r[:, 1], r[:, 2])
            y0 = jnp.full_like(x, 0.5 / sqrt(pi))[:, None]
            c1 = sqrt(3.0 / (4.0 * pi))
            y1 = c1 * jnp.stack([y, z, x], axis=-1)
            c2a = 0.5 * sqrt(15.0 / pi)
            c2b = 0.25 * sqrt(5.0 / pi)
            c2c = 0.25 * sqrt(15.0 / pi)
            y2 = jnp.stack([c2a * x * y, c2a * y * z, c2b * (3.0 * z * z - 1.0), c2a * x * z, c2c * (x * x - y * y)], axis=-1)
            return jnp.concatenate([y0, y1, y2], axis=-1)
        key = jax.random.key(seed)
        ks = jax.random.split(key, 6)
        features = jax.random.normal(ks[0], (N_NODES, FEAT_DIM), dtype=jnp.float32)
        abs_distances = jax.random.uniform(ks[1], (N_EDGES,), dtype=jnp.float32, minval=0.1, maxval=1.0)
        rel_vec = jax.random.normal(ks[2], (N_EDGES, 3), dtype=jnp.float32)
        edge_index = jax.random.randint(ks[3], (2, N_EDGES), 0, N_NODES, dtype=jnp.int32)
        w1 = jax.random.normal(ks[4], (1, HIDDEN), dtype=jnp.float32)
        b1 = jnp.zeros((HIDDEN,), jnp.float32)
        w2 = jax.random.normal(ks[5], (HIDDEN, R_DIM), dtype=jnp.float32) / sqrt(HIDDEN)
        b2 = jnp.zeros((R_DIM,), jnp.float32)
        return {'features': features, 'abs_distances': abs_distances, 'rel_vec': rel_vec, 'edge_index': edge_index, 'w1': w1, 'b1': b1, 'w2': w2, 'b2': b2}
    _L1_gnn_all = _L1_gnn_setup()
    _L1_gnn_in = {k: v for k, v in _L1_gnn_all.items() if k in ('w1', 'b1', 'w2', 'b2')}
    del _L1_gnn_all
    return {'x': x, 'src': src, 'dst': dst, 'edge_attr_3': edge_attr_3, 'edge_weight': edge_weight, 'edge_weight1': edge_weight1, 'L0_gnn_W1': _L0_gnn_in['W1'], 'L0_gnn_b1': _L0_gnn_in['b1'], 'L0_gnn_W2': _L0_gnn_in['W2'], 'L0_gnn_b2': _L0_gnn_in['b2'], 'L0_gnn_W3': _L0_gnn_in['W3'], 'L0_gnn_b3': _L0_gnn_in['b3'], 'L0_gnn_W4': _L0_gnn_in['W4'], 'L0_gnn_b4': _L0_gnn_in['b4'], 'L1_gnn_w1': _L1_gnn_in['w1'], 'L1_gnn_b1': _L1_gnn_in['b1'], 'L1_gnn_w2': _L1_gnn_in['w2'], 'L1_gnn_b2': _L1_gnn_in['b2']}

def reference(x, src, dst, edge_attr_3, edge_weight, edge_weight1, L0_gnn_W1, L0_gnn_b1, L0_gnn_W2, L0_gnn_b2, L0_gnn_W3, L0_gnn_b3, L0_gnn_W4, L0_gnn_b4, L1_gnn_w1, L1_gnn_b1, L1_gnn_w2, L1_gnn_b2):
    import jax
    import jax.numpy as jnp

    def _L0_gnn_ref(inputs, e, edge_index, W1, b1, W2, b2, W3, b3, W4, b4):
        import jax, jax.numpy as jnp
        import numpy as np
        N = 50000
        E = 25000
        D = 32
        H = 32
        x = inputs
        src = edge_index[0]
        dst = edge_index[1]
        ex1 = e * x[src]
        ex2 = e * x[dst]
        mi = jnp.zeros_like(x).at[dst].add(ex1)
        mo = jnp.zeros_like(x).at[src].add(ex2)
        h = jnp.concatenate([mi, mo, x], axis=1)
        h = jnp.tanh(h @ W1 + b1)
        h = jnp.tanh(h @ W2 + b2)
        h = jnp.tanh(h @ W3 + b3)
        return jnp.tanh(h @ W4 + b4)

    def _L1_gnn_ref(features, abs_distances, rel_vec, edge_index, w1, b1, w2, b2):
        import jax, jax.numpy as jnp
        import numpy as np
        from math import factorial, pi, sqrt
        MUL = 8
        RS = [(MUL, 0), (MUL, 1)]
        N_NODES = 20000
        N_EDGES = 10000
        FEAT_DIM = sum((m * (2 * l + 1) for m, l in RS))
        R_DIM = sum((mo * mi * (2 * min(lo, li) + 1) for mo, lo in RS for mi, li in RS))
        HIDDEN = 64

        def _cg(j1, j2, j3, m1, m2, m3):
            if m1 + m2 != m3:
                return 0.0
            f = factorial
            pre = sqrt((2 * j3 + 1) * f(j3 + j1 - j2) * f(j3 - j1 + j2) * f(j1 + j2 - j3) / f(j1 + j2 + j3 + 1))
            pre *= sqrt(f(j3 + m3) * f(j3 - m3) * f(j1 - m1) * f(j1 + m1) * f(j2 - m2) * f(j2 + m2))
            kmin = max(0, j2 - j3 - m1, j1 - j3 + m2)
            kmax = min(j1 + j2 - j3, j1 - m1, j2 + m2)
            s = 0.0
            for k in range(kmin, kmax + 1):
                s += (-1) ** k / (f(k) * f(j1 + j2 - j3 - k) * f(j1 - m1 - k) * f(j2 + m2 - k) * f(j3 - j2 + m1 + k) * f(j3 - j1 - m2 + k))
            return pre * s

        def _w3j_complex(l1, l2, l3):
            w = np.zeros((2 * l1 + 1, 2 * l2 + 1, 2 * l3 + 1))
            for m1 in range(-l1, l1 + 1):
                for m2 in range(-l2, l2 + 1):
                    m3 = -(m1 + m2)
                    if abs(m3) <= l3:
                        w[m1 + l1, m2 + l2, m3 + l3] = (-1) ** (l1 - l2 - m3) / sqrt(2 * l3 + 1) * _cg(l1, l2, l3, m1, m2, -m3)
            return w

        def _A(l):
            A = np.zeros((2 * l + 1, 2 * l + 1), dtype=complex)
            A[l, l] = 1.0
            for m in range(1, l + 1):
                A[l + m, l + m] = (-1) ** m / sqrt(2)
                A[l + m, l - m] = 1.0 / sqrt(2)
                A[l - m, l - m] = 1j / sqrt(2)
                A[l - m, l + m] = -1j * (-1) ** m / sqrt(2)
            return A

        def real_w3j(l1, l2, l3):
            wc = _w3j_complex(l1, l2, l3).astype(complex)
            wr = np.einsum('abc,ma,nb,oc->mno', wc, _A(l1).conj(), _A(l2).conj(), _A(l3).conj())
            i = int(np.argmax(np.abs(wr)))
            ph = wr.flat[i] / abs(wr.flat[i])
            wr = wr / ph
            assert np.abs(wr.imag).max() < 1e-10
            return np.real(wr).astype(np.float32)
        _W3J = {}
        for _mo, _lo in RS:
            for _mi, _li in RS:
                for _lf in range(abs(_lo - _li), _lo + _li + 1):
                    if (_lo, _lf, _li) not in _W3J:
                        _W3J[_lo, _lf, _li] = jnp.asarray(real_w3j(_lo, _lf, _li))
        _NORM = []
        for _mo, _lo in RS:
            _num = sum((mi * (2 * min(_lo, li) + 1) for mi, li in RS))
            _NORM.append(sqrt(4.0 * pi) * sqrt(2.0 * _lo + 1.0) / sqrt(_num))
        _F_OFFS = [0] + list(np.cumsum([mi * (2 * li + 1) for mi, li in RS]))

        def spherical_harmonics(rel_vec):
            r = rel_vec / jnp.linalg.norm(rel_vec, axis=-1, keepdims=True)
            x, y, z = (r[:, 0], r[:, 1], r[:, 2])
            y0 = jnp.full_like(x, 0.5 / sqrt(pi))[:, None]
            c1 = sqrt(3.0 / (4.0 * pi))
            y1 = c1 * jnp.stack([y, z, x], axis=-1)
            c2a = 0.5 * sqrt(15.0 / pi)
            c2b = 0.25 * sqrt(5.0 / pi)
            c2c = 0.25 * sqrt(15.0 / pi)
            y2 = jnp.stack([c2a * x * y, c2a * y * z, c2b * (3.0 * z * z - 1.0), c2a * x * z, c2c * (x * x - y * y)], axis=-1)
            return jnp.concatenate([y0, y1, y2], axis=-1)
        src, dst = (edge_index[0], edge_index[1])
        R = jax.nn.relu(abs_distances[:, None] @ w1 + b1) @ w2 + b2
        Y = spherical_harmonics(rel_vec)
        Fj = features[src]
        E = Fj.shape[0]
        msg_blocks = []
        r_off = 0
        for i, (mo, lo) in enumerate(RS):
            acc = jnp.zeros((E, mo, 2 * lo + 1), dtype=features.dtype)
            for j, (mi, li) in enumerate(RS):
                n_lf = 2 * min(lo, li) + 1
                sz = mo * mi * n_lf
                Rb = R[:, r_off:r_off + sz].reshape(E, mo, mi, n_lf)
                r_off += sz
                Fb = Fj[:, _F_OFFS[j]:_F_OFFS[j + 1]].reshape(E, mi, 2 * li + 1)
                for k, lf in enumerate(range(abs(lo - li), lo + li + 1)):
                    C = _W3J[lo, lf, li]
                    Yf = Y[:, lf * lf:(lf + 1) * (lf + 1)]
                    acc = acc + _NORM[i] * jnp.einsum('euv,ef,evi,ofi->euo', Rb[..., k], Yf, Fb, C)
            msg_blocks.append(acc.reshape(E, -1))
        msg = jnp.concatenate(msg_blocks, axis=-1)
        out = jnp.zeros((features.shape[0], msg.shape[1]), dtype=features.dtype)
        out = out.at[dst].add(msg)
        return out
    edge_index = jnp.stack([src, dst])
    x = _layernorm(x + _L0_gnn_ref(x, edge_weight1, edge_index, L0_gnn_W1, L0_gnn_b1, L0_gnn_W2, L0_gnn_b2, L0_gnn_W3, L0_gnn_b3, L0_gnn_W4, L0_gnn_b4), axis=-1)
    x = _layernorm(x + _L1_gnn_ref(x, edge_weight, edge_attr_3, edge_index, L1_gnn_w1, L1_gnn_b1, L1_gnn_w2, L1_gnn_b2), axis=-1)
    return x

_drawn_inputs = setup_inputs


def setup_inputs(seed=0):
    import zlib

    import numpy as np

    out = dict(_drawn_inputs(seed))
    spreads = {'L0_gnn_b1': (0.0, 0.8),
     'L0_gnn_b2': (0.0, 0.8),
     'L0_gnn_b3': (0.0, 0.339),
     'L0_gnn_b4': (0.0, 0.1),
     'L1_gnn_b1': (0.0, 0.289),
     'L1_gnn_b2': (0.0, 0.1)}
    factors = {'edge_weight1': 8.0, 'L0_gnn_W1': 8.0, 'L0_gnn_W2': 8.0, 'L0_gnn_W3': 6.836}
    for name, (base, spread) in spreads.items():
        noise = np.random.default_rng([zlib.crc32(name.encode()), seed]).standard_normal(out[name].shape)
        drawn = base * np.exp(spread * noise) if base else spread * noise
        out[name] = jnp.asarray(drawn.astype(out[name].dtype))
    for name, factor in factors.items():
        out[name] = (out[name] * factor).astype(out[name].dtype)
    return out
```

```python
from contextlib import ExitStack
from math import sqrt

import concourse.bass as bass
from concourse import mybir

F32 = mybir.dt.float32
I32 = mybir.dt.int32
ALU = mybir.AluOpType
ACT = mybir.ActivationFunctionType
AX_X = mybir.AxisListType.X

P = 128
N, E, D = 100000, 25000, 32
J = 4
WIN = P * J
NW = -(-N // WIN)
NPAD = NW * WIN
NT = -(-E // P)
U = 7
NG = NT // U
HALF = NT // 2
BW = 4
NB = NW // BW
BC = BW * P
PAD_NODE = N + P
EPS = 1e-5
AHEAD = 4
HID, RC = 64, 384
assert NT == NW and NG * U == NT and NG % 2 == 0 and NB * BW == NW and NB % 2 == 1
assert PAD_NODE + NT * P - E <= NPAD

C_00 = 0.25
C_10 = sqrt(3.0 / 32.0)
C_11_0 = sqrt(1.0 / 32.0)
C_11_1 = sqrt(3.0 / 64.0)
C_11_2 = 0.375


def count(g, per, off=0):
    i, k = g
    return i * (2 * per) + (k * per + off)


def slot_count(g, per):
    i, k = g
    return i * per + (k // 2 + 1) * per


def wait(eng, sem, value):
    if isinstance(value, int) and value <= 0:
        return
    eng.wait_ge(sem, value)


def over_pairs(eng, step, n):
    step((0, 0))
    step((0, 1))
    with eng.Fori(0, n // 2 - 1) as i:
        step((i, 2))
        step((i, 3))
    if n % 2:
        step((n // 2 - 1, 2))


def staged(eng, stages, n):
    lag = len(stages)

    def step(s, ends=False):
        for k in reversed(range(lag)):
            if stages[k] and (not ends or 0 <= s[1] - k < n):
                stages[k]((s[0], s[1] - k))

    peeled = lag + 1 + (lag + 1) % 2
    pairs = (n - peeled) // 2
    for s in range(peeled):
        step((0, s), ends=True)
    with eng.Fori(0, pairs) as i:
        step((i, peeled))
        step((i, peeled + 1))
    for s in range(peeled + 2 * pairs, n + lag - 1):
        step((0, s), ends=True)


def act_copy(act, out, in_):
    return act.activation(out, in_, ACT.Copy)


def wait_here(pool, sem, value, passed):
    if isinstance(value, int):
        return wait(pool, sem, value)
    pool.wait_ge(sem, value)
    pool.sem_inc(passed, 1)


class Chain:

    def __init__(self, eng, sem, per):
        self.eng, self.sem, self.per = eng, sem, per

    def begin(self, g):
        self.g, self.n = g, 0

    def mark(self, instruction):
        instruction.then_inc(self.sem, 1)
        self.n += 1

    def need(self, back=0):
        wait(self.eng, self.sem, count(self.g, self.per, self.n - back))

    def end(self):
        assert self.n == self.per, (self.n, self.per)


def gnn_kernel(nc, x, src, dst, ea, ew, ew1, W1, b1, W2, b2, W3, b3, W4, b4, rw1, rb1, rw2, rb2, out):
    x_w = x.rearrange("(w p j) f -> p w (j f)", p=P, j=J)
    out_w = out.rearrange("(w p j) f -> p w (j f)", p=P, j=J)

    def dram(name):
        return nc.dram_tensor(name, (NPAD, D), F32, kind="Internal").ap()

    def windows(a):
        return a.rearrange("(w p j) f -> p w (j f)", p=P, j=J)

    acc_in, acc_out, xc_d, x1_d = dram("acc_in"), dram("acc_out"), dram("xc_d"), dram("x1_d")
    acc_l1 = [dram("acc_l1a"), dram("acc_l1b")]

    with ExitStack() as ctx:
        def sb(name, shape, dt=F32):
            return ctx.enter_context(nc.sbuf_tensor(name, shape, dt))

        phase_1, phase_2 = ExitStack(), ExitStack()

        def sb1(name, shape, dt=F32):
            return phase_1.enter_context(nc.sbuf_tensor(name, shape, dt))

        def sb2(name, shape, dt=F32):
            return phase_2.enter_context(nc.sbuf_tensor(name, shape, dt))

        def sem(name):
            return ctx.enter_context(nc.semaphore(name))

        def pair(make, name, *a):
            return [make(f"{name}{h}", *a) for h in range(2)]

        res = sb("res", [P, NW, P])
        ident = sb("ident", [P, P])
        lower = sb("lower", [P, P])
        zeros = sb("zeros", [P, 512])
        tr_i = sb("tr_i", [P, 1], I32)
        tr_f = sb("tr_f", [P, 1])
        key_f = sb("key_f", [P, 2, NT])
        key_i = sb("key_i", [P, 2, NT + 2 * U], I32)
        to_spare = sb("to_spare", [P, 2, NT])
        w1e = sb("w1e", [P, NT])
        dir5 = sb("dir5", [P, NT, 5])
        sdst_all = sb("sdst_all", [P, NT + U], I32)
        w1ab = sb("w1ab", [2 * D, D])
        w1c = sb("w1c", [P, P])
        wl = [sb(f"wl{n}", [P, P]) for n in range(3)]
        centre = sb("centre", [P, P])
        centred = sb("centred", [P, P])
        bias = sb("bias", [P, 4])
        rw1c = sb("rw1c", [HID, 2])
        rw_raw = sb("rw_raw", [HID + 1, RC])
        rw = sb("rw", [HID + 1, 24, 16])
        rw_t = sb("rw_t", [HID + 1, 8, 8])

        rows_d = pair(sb, "rows_d", [P, U, P], I32)
        gidx = pair(sb, "gidx", [P, 2, U], I32)
        sidx = pair(sb, "sidx", [P, 2, U], I32)
        gat = pair(sb, "gat", [P, 2, U, D])
        same = sb("same", [P, 2, U, P])

        idx_rows = sb1("idx_rows", [HALF, 2, 2, P], I32)
        val_rows = sb1("val_rows", [HALF, 6, 2, P])
        ea_rows = sb1("ea_rows", [HALF, 2, P * 3])
        rel = sb1("rel", [P, NT, 3])
        relsq = sb1("relsq", [P, NT, 3])
        rnorm = sb1("rnorm", [P, NT])
        rsum = sb1("rsum", [P, NT])
        rinv = sb1("rinv", [P, NT])
        rows_s = pair(sb1, "rows_s", [P, U, P], I32)
        wmsg = sb1("wmsg", [P, 2, U, D])
        earlier = sb1("earlier", [P, 2, U, P])
        dups = sb1("dups", [P, 2, U])
        spare_step = sb1("spare_step", [P, 2, U])
        row_f = sb1("row_f", [P, 2, U])
        msg_t = sb1("msg_t", [2 * D, U, P])
        pay = pair(sb1, "pay", [P, 2, U, D])
        xw = pair(sb1, "xw", [P, U, P])
        xt = sb1("xt", [P, U, P])
        xmean = sb1("xmean", [P, U * J])
        xcen = pair(sb1, "xcen", [P, U, P])
        phase_1.close()

        ld_a = pair(sb, "ld_a", [P, BC])
        ld_b = pair(sb, "ld_b", [P, BC])
        ld_c = pair(sb, "ld_c", [P, BC])
        pre = pair(sb, "pre", [P, BC])
        ysq = pair(sb, "ysq", [P, BC])
        ssq = sb("ssq", [P, BW * J])
        vps = sb("vps", [P, BW * J])
        rstd = sb("rstd", [P, BW * J])
        var = sb("var", [P, NB, BW * J])
        dev = sb("dev", [P, NB, BW * J])
        rsd = sb("rsd", [P, NB, BW * J])
        newton = pair(sb, "newton", [P, BW * J])

        hid = [pair(sb2, f"hid{n}_", [P, BC]) for n in range(4)]
        phase_2.close()

        arow = pair(sb, "arow", [HID, U * P])
        ht = pair(sb, "ht", [HID + 1, U * P])
        feat5 = sb("feat5", [P, U, 8, 5])
        fd = pair(sb, "fd", [P, U, 2, 8])
        fk = pair(sb, "fk", [P, U, 3, 2, 8])
        dprod = sb("dprod", [P, U, 8, 3])
        kp = sb("kp", [P, 2, U, 8, 3])
        prod_s = pair(sb, "prod_s", [P, 16, 16])
        prod_v = pair(sb, "prod_v", [P, 8, 3, 16])
        red_s = sb("red_s", [P, U, 16])
        red_v = sb("red_v", [P, U, 8, 3])
        rq = sb("rq", [P, U, 8, 3])
        msg1 = pair(sb, "msg1", [P, U, D])
        pay1 = pair(sb, "pay1", [P, U, D])

        psum = [ctx.enter_context(nc.psum_tensor(f"bank{n}", [P, 512], F32)) for n in range(8)]

        def two_banks(n):
            return lambda k: psum[n + k // 4][:, (k % 4) * P:(k % 4 + 1) * P]

        s_const = sem("s_const")
        s_fill = sem("s_fill")
        s_wld = sem("s_wld")
        s_first = sem("s_first")
        s_eld = sem("s_eld")
        s_zero = sem("s_zero")
        s_zero1 = sem("s_zero1")
        s_erow = sem("s_erow")
        s_ecol = sem("s_ecol")
        s_prep = sem("s_prep")
        s_passed = sem("s_passed")
        s_sum = sem("s_sum")
        s_norm = sem("s_norm")
        s_ready = sem("s_ready")
        s_wchain = sem("s_wchain")
        s_wprep = sem("s_wprep")

        block = ctx.enter_context(nc.Block())

        a_rows = pair(sem, "a_rows")
        a_xw = pair(sem, "a_xwin")
        a_xst = pair(sem, "a_xst")
        a_idx = sem("a_idx")
        a_gat = pair(sem, "a_gat")
        a_same = sem("a_same")
        a_sidx = sem("a_sidx")
        a_xcen = sem("a_xcen")
        a_wmsg = sem("a_wmsg")
        a_dve = sem("a_dve")
        a_xt_p = sem("a_xt_p")
        a_msg_p = sem("a_msg_p")
        a_xw1_p = sem("a_xw1_p")
        a_pay_p = sem("a_pay_p")
        a_xt = sem("a_xt")
        a_msg = sem("a_msg")
        a_xw1 = sem("a_xw1")
        a_pay = sem("a_pay")
        a_sc = [sem("a_sc_in"), sem("a_sc_out")]

        m_ld = pair(sem, "m_ld")
        m_xc = pair(sem, "m_xc")
        m_sum1 = sem("m_sum1")
        m_pre = sem("m_pre")
        m_mm = [sem(f"m_mm{n}") for n in range(5)]
        m_act = [sem(f"m_act{n}") for n in range(4)]
        m_y = sem("m_y")
        m_sq = sem("m_sq")
        m_ssq = sem("m_ssq")
        m_dve = sem("m_dve")
        m_x1 = sem("m_x1")
        m_st = sem("m_st")

        c_rows = pair(sem, "c_rows")
        c_arow = pair(sem, "c_arow")
        c_ones = sem("c_ones")
        c_gidx = sem("c_gidx")
        c_sidx = sem("c_sidx")
        c_red = sem("c_red")
        c_gat = pair(sem, "c_gat")
        c_same = sem("c_same")
        c_dve = sem("c_dve")
        c_feat = sem("c_feat")
        c_fk = sem("c_fk")
        c_ht = sem("c_ht")
        c_r = sem("c_r")
        c_use = sem("c_use")
        c_msg = sem("c_msg")
        c_pay_p = sem("c_pay_p")
        c_pay = sem("c_pay")
        c_sc = [sem("c_sc_a"), sem("c_sc_b")]

        z_ld = pair(sem, "z_ld")
        z_n = sem("z_n")
        z_sum = sem("z_sum")
        z_dve = sem("z_dve")
        z_y = sem("z_y")
        z_sq = sem("z_sq")
        z_var = sem("z_var")
        z_root = sem("z_root")
        z_r = sem("z_r")
        z_out = sem("z_out")
        z_st = pair(sem, "z_st")

        def wins(a):
            return a.rearrange("p (w c) -> p w c", w=BW)

        def nodes(a):
            return a.rearrange("p (n f) -> p n f", f=D)

        def batch(b):
            return res[:, bass.ds(count(b, BW), BW), :]

        def rows(b):
            return batch(b).rearrange("p w (j f) -> p (w j) f", f=D)

        def small(a, b):
            return a[:, bass.ds(count(b, 1), 1), :].rearrange("p o n -> p (o n)")

        def landed_3(g, c, more=0):
            i, k = g
            in_pair = [(h + t) % 2 for h in range(k % 2 + 1) for t in range(U)].count(c)
            return i * (16 * U) + 16 * ((k // 2) * U + in_pair + more)

        N_WLD = 16 * (8 * J + 5)

        @block.sync
        def _(sp):
            half = lambda a: a.rearrange("(c r) q -> r c q", c=2)
            sp.dma_start(idx_rows[:, 0], half(src)).then_inc(s_eld, 16)
            sp.dma_start(idx_rows[:, 1], half(dst)).then_inc(s_eld, 16)
            sp.dma_start(val_rows[:, 2], half(ew1)).then_inc(s_eld, 16)
            sp.dma_start(ea_rows[:, :, :], half(ea)).then_inc(s_eld, 16)
            sp.wait_ge(s_fill, 6)

            def load_1(g):
                h = g[1] % 2
                t0 = count(g, U)
                wait(sp, a_same, count(g, 2, -2))
                for rows, a in ((rows_s[h], src), (rows_d[h], dst)):
                    sp.dma_start(rows[:, :, :], a[bass.ds(t0, U), :].partition_broadcast(P)).then_inc(a_rows[h], 16)
                wait(sp, a_xt_p, count(g, 1, -1))
                wait(sp, a_xcen, count(g, 1, -1))
                sp.dma_start(xw[h][:, :, :], x_w[:, bass.ds(t0, U), :]).then_inc(a_xw[h], 16)

            sp.wait_ge(s_eld, 64)
            sp.sem_inc(s_first, 1)
            load_1((0, 0))
            for n, wt in enumerate((W1[2 * D:3 * D, :], W2, W3, W4)):
                for j in range(J):
                    s = slice(D * j, D * j + D)
                    sp.dma_start((w1c, *wl)[n][s, s], wt).then_inc(s_wld, 16)
            for n, b in enumerate((b1, b2, b3, b4)):
                for j in range(J):
                    sp.dma_start(bias[D * j:D * j + D, n:n + 1], b).then_inc(s_wld, 16)
            sp.dma_start(w1ab[:, :], W1[0:2 * D, :]).then_inc(s_wld, 16)
            sp.dma_start(rw1c[:, 0:1], rw1).then_inc(s_wld, 16)
            sp.dma_start(rw1c[:, 1:2], rb1).then_inc(s_wld, 16)
            sp.dma_start(rw_raw[0:HID, :], rw2).then_inc(s_wld, 16)
            sp.dma_start(rw_raw[HID:HID + 1, :], rb2).then_inc(s_wld, 16)

            def store_1(g):
                h = g[1] % 2
                sp.wait_ge(a_xcen, count(g, 1, 1))
                sp.dma_start(windows(xc_d)[:, bass.ds(count(g, U), U), :], xcen[h][:, :, :]).then_inc(a_xst[h], 16)

            def clear_1(g):
                for a in acc_l1:
                    sp.dma_start(windows(a)[:, bass.ds(count(g, U), U), :],
                                 zeros[:, 0:P].unsqueeze(1).broadcast_to([P, U, P])).then_inc(s_zero1, 16)

            def step_1(g):
                load_1((g[0], g[1] + 1))
                store_1(g)
                clear_1(g)

            step_1((0, 0))
            with sp.Fori(0, NG // 2 - 1) as i:
                step_1((i, 1))
                step_1((i, 2))
            store_1((0, NG - 1))
            clear_1((0, NG - 1))
            for h in range(2):
                sp.wait_ge(a_xst[h], 16 * NG // 2)
            for s in a_sc:
                sp.wait_ge(s, 16 * NT)

            def load_2(b):
                h = b[1] % 2
                ws = bass.ds(count(b, BW), BW)
                wait(sp, m_pre, count(b, 1, -1))
                for buf, a in ((ld_a[h], acc_in), (ld_b[h], acc_out)):
                    sp.dma_start(buf[:, :].rearrange("p (w c) -> p w c", w=BW), windows(a)[:, ws, :]).then_inc(m_ld[h], 16)

            def load_xc_2(b):
                h = b[1] % 2
                ws = bass.ds(count(b, BW), BW)
                wait(sp, m_y, count(b, 1, -1))
                sp.dma_start(ld_c[h][:, :].rearrange("p (w c) -> p w c", w=BW), windows(xc_d)[:, ws, :]).then_inc(m_xc[h], 16)

            def store_2(b):
                ws = bass.ds(count(b, BW), BW)
                sp.wait_ge(m_x1, count(b, 1, 1))
                sp.dma_start(windows(x1_d)[:, ws, :], res[:, ws, :]).then_inc(m_st, 16)

            staged(sp, [load_2, None, None, None, None, load_xc_2] + [None] * 4 + [store_2], NB)

            def load_3(g):
                h = g[1] % 2
                t0 = count(g, U)
                wait(sp, c_same, count(g, 1, -1))
                sp.dma_start(rows_d[h][:, :, :], dst[bass.ds(t0, U), :].partition_broadcast(P)).then_inc(c_rows[h], 16)
                wait(sp, c_ht, count(g, 1, -1))
                sp.dma_start(arow[h][:, :].rearrange("p (t q) -> p t q", t=U),
                             ew[bass.ds(t0, U), :].partition_broadcast(HID)).then_inc(c_arow[h], 16)

            over_pairs(sp, load_3, NG)
            for s in c_sc:
                sp.wait_ge(s, 16 * NT // 2)

            def load_4(b):
                h = b[1] % 2
                wait(sp, z_sum, count(b, 1, -1))
                for buf, a in ((ld_a[h], acc_l1[0]), (ld_b[h], acc_l1[1])):
                    sp.dma_start(buf[:, :].rearrange("p (w c) -> p w c", w=BW),
                                 windows(a)[:, bass.ds(count(b, BW), BW), :]).then_inc(z_ld[h], 16)

            def store_4(b):
                h = b[1] % 2
                sp.wait_ge(z_out, count(b, 1, 1))
                sp.dma_start(out_w[:, bass.ds(count(b, BW), BW), :],
                             ysq[h][:, :].rearrange("p (w c) -> p w c", w=BW)).then_inc(z_st[h], 16)

            staged(sp, [load_4] + [None] * 7 + [store_4], NB)
            sp.wait_ge(z_st[0], 16 * (NB // 2 + 1))
            sp.wait_ge(z_st[1], 16 * (NB // 2))

        @block.gpsimd
        def _(pool):
            pool.memset(ident[:, :], 0.0).then_inc(s_const, 1)
            pool.memset(lower[:, :], 1.0).then_inc(s_const, 1)
            pool.iota(tr_i[:, :], [[0, 1]], base=N, channel_multiplier=1).then_inc(s_const, 1)
            pool.wait_ge(s_const, 3)
            pool.affine_select(out=ident[:, :], in_=ident[:, :], compare_op=ALU.not_equal, fill=1.0, base=0,
                               pattern=[[-1, P]], channel_multiplier=1).then_inc(s_const, 1)
            pool.affine_select(out=lower[:, :], in_=lower[:, :], compare_op=ALU.is_gt, fill=0.0, base=0,
                               pattern=[[-1, P]], channel_multiplier=1).then_inc(s_const, 1)

            def gather(h, c, k, table, sem_):
                pool.indirect_dma_start(gat[h][:, c, k, :], None, table,
                                        bass.IndirectOffsetOnAxis(ap=gidx[h][:, c, k:k + 1], axis=0)).then_inc(sem_, 16)

            def scatter_1(g, c, k):
                h = g[1] % 2
                wait_here(pool, a_sc[c], count(g, 16 * U, 16 * k), s_passed)
                pool.indirect_dma_start((acc_in, acc_out)[c], bass.IndirectOffsetOnAxis(ap=sidx[h][:, 1 - c, k:k + 1], axis=0),
                                        pay[h][:, c, k, :], None, compute_op=ALU.add).then_inc(a_sc[c], 16)

            def ready_1(g):
                wait_here(pool, a_pay, count(g, 1, 1), s_passed)
                wait_here(pool, a_sidx, count(g, 1, 1), s_passed)

            def step_1(g, first=False):
                h = g[1] % 2
                before = (g[0], g[1] - 2)
                wait_here(pool, a_idx, count(g, 1, 1), s_passed)
                wait_here(pool, a_wmsg, count(g, 1, -1), s_passed)
                for k in range(U):
                    gather(h, 0, k, x, a_gat[h])
                    if not first:
                        if k == 0:
                            ready_1(before)
                        scatter_1(before, 0, k)
                    gather(h, 1, k, x, a_gat[h])
                    if not first:
                        scatter_1(before, 1, k)

            step_1((0, 0), first=True)
            step_1((0, 1), first=True)
            pool.wait_ge(s_zero, 32)
            step_1((0, 2))
            step_1((0, 3))
            with pool.Fori(0, NG // 2 - 2) as i:
                step_1((i, 4))
                step_1((i, 5))
            for g in (NG - 2, NG - 1):
                ready_1((0, g))
                for k in range(U):
                    scatter_1((0, g), 0, k)
                    scatter_1((0, g), 1, k)
            for s in a_sc:
                pool.wait_ge(s, 16 * NT)

            pool.wait_ge(a_xw1, 2 * NG)

            def step_2(b):
                h = b[1] % 2
                pool.wait_ge(m_ld[h], slot_count(b, 32))
                wait(pool, m_mm[0], count(b, 1, -1))
                pool.tensor_tensor(ld_a[h][:, :], ld_a[h][:, :], ld_b[h][:, :], ALU.add).then_inc(m_sum1, 1)
                pool.wait_ge(m_sum1, count(b, 1, 1))
                pool.tensor_tensor(pre[h][:, :].rearrange("p (w c) -> p w c", w=BW), ld_a[h][:, :].rearrange("p (w c) -> p w c", w=BW),
                                   res[:, bass.ds(count(b, BW), BW), :], ALU.add).then_inc(m_pre, 1)

            over_pairs(pool, step_2, NB)

            def scatter_3(g, k):
                h = g[1] % 2
                c = (h + k) % 2
                earlier_3 = [(h + a) % 2 for a in range(k)].count(c)
                wait_here(pool, c_sc[c], landed_3((g[0], g[1] - 1), c, earlier_3), s_passed)
                pool.indirect_dma_start(acc_l1[c], bass.IndirectOffsetOnAxis(ap=sidx[h][:, 0, k:k + 1], axis=0),
                                        pay1[h][:, k, :], None, compute_op=ALU.add).then_inc(c_sc[c], 16)

            def step_3(g, first=False):
                h = g[1] % 2
                before = (g[0], g[1] - 2)
                wait_here(pool, c_gidx, count(g, 1, 1), s_passed)
                wait_here(pool, c_fk, count(g, 1, -1), s_passed)
                for k in range(U + AHEAD):
                    if k < U:
                        gather(h, 0, k, x1_d, c_gat[h])
                    if not first and k >= AHEAD:
                        if k == AHEAD:
                            wait_here(pool, c_pay, count(before, 1, 1), s_passed)
                            wait_here(pool, c_sidx, count(before, 1, 1), s_passed)
                        scatter_3(before, k - AHEAD)

            pool.wait_ge(m_st, 16 * NB)
            pool.wait_ge(s_zero1, 16 * 2 * NG)
            step_3((0, 0), first=True)
            step_3((0, 1), first=True)
            step_3((0, 2))
            step_3((0, 3))
            with pool.Fori(0, NG // 2 - 2) as i:
                step_3((i, 4))
                step_3((i, 5))
            pool.wait_ge(c_pay, NG)
            pool.wait_ge(c_sidx, NG)
            for g in (NG - 2, NG - 1):
                for k in range(U):
                    scatter_3((0, g), k)
            for s in c_sc:
                pool.wait_ge(s, 16 * NT // 2)

            def add_4(b):
                h = b[1] % 2
                pool.wait_ge(z_ld[h], slot_count(b, 32))
                wait(pool, z_y, count(b, 1, -1))
                pool.tensor_tensor(pre[h][:, :], ld_a[h][:, :], ld_b[h][:, :], ALU.add).then_inc(z_sum, 1)

            def norm_4(b):
                h = b[1] % 2
                pool.wait_ge(z_r, count(b, 1, 1))
                wait(pool, z_st[h], slot_count(b, 16) - 16)
                pool.tensor_tensor(nodes(ysq[h][:, :]), rows(b), small(rsd, b).unsqueeze(2).broadcast_to([P, BW * J, D]),
                                   ALU.mult).then_inc(z_out, 1)

            staged(pool, [add_4] + [None] * 5 + [norm_4], NB)

        @block.scalar
        def _(act):
            def clear(accs, done):
                for a in accs:
                    act.dma_start(a.rearrange("(p a c) f -> p a (c f)", p=P, c=16),
                                  zeros[:, :].unsqueeze(1).broadcast_to([P, NPAD // P // 16, 512])).then_inc(done, 16)

            act.wait_ge(s_fill, 1)
            act.wait_ge(s_first, 1)
            clear((acc_in, acc_out), s_zero)
            act.wait_ge(s_sum, 1)
            act.activation(rnorm[:, :], rsum[:, :], ACT.Sqrt).then_inc(s_norm, 1)
            act.wait_ge(s_wld, N_WLD)

            def step_1(g):
                h = g[1] % 2
                act.wait_ge(a_xt_p, count(g, 1, 1))
                wait(act, a_xw1_p, count(g, 1))
                act_copy(act, xt[:, 0:4, :], psum[0][:, :]).then_inc(a_xt, 1)
                act_copy(act, xt[:, 4:U, :], psum[1][:, 0:3 * P]).then_inc(a_xt, 1)
                act.wait_ge(a_msg_p, count(g, 1, 1))
                wait(act, a_pay_p, count(g, 1))
                act_copy(act, msg_t[:, 0:4, :], psum[2][0:2 * D, :]).then_inc(a_msg, 1)
                act_copy(act, msg_t[:, 4:U, :], psum[3][0:2 * D, 0:3 * P]).then_inc(a_msg, 1)
                act.wait_ge(a_xw1_p, count(g, 1, 1))
                w0 = count(g, U)
                act_copy(act, res[:, bass.ds(w0, 4), :], psum[4][:, :].rearrange("p (w c) -> p w c", w=4)).then_inc(a_xw1, 1)
                act_copy(act, res[:, bass.ds(w0 + 4, 3), :], psum[5][:, 0:3 * P].rearrange("p (w c) -> p w c", w=3)).then_inc(a_xw1, 1)
                act.wait_ge(a_pay_p, count(g, 1, 1))
                for s in a_sc:
                    wait(act, s, count(g, 16 * U, -16 * U))
                act_copy(act, pay[h][:, 0], psum[6][:, 0:U * D].rearrange("p (t f) -> p t f", t=U))
                act_copy(act, pay[h][:, 1], psum[7][:, 0:U * D].rearrange("p (t f) -> p t f", t=U)).then_inc(a_pay, 1)

            over_pairs(act, step_1, NG)

            def tanh(n, b):
                h = b[1] % 2
                act.wait_ge(m_mm[n], count(b, 1, 1))
                wait(act, m_mm[n + 1], count(b, 1, -1))
                act.activation(hid[n][h][:, :], psum[n][:, :], ACT.Tanh, bias=bias[:, n:n + 1]).then_inc(m_act[n], 1)

            def square_2(b):
                h = b[1] % 2
                act.wait_ge(m_y, count(b, 1, 1))
                wait(act, m_ssq, count(b, 1, -1))
                act.activation(wins(ysq[h][:, :]), batch(b), ACT.Square, scale=D ** -0.5).then_inc(m_sq, 1)

            staged(act, [lambda b, n=n: tanh(n, b) for n in range(4)] + [None, square_2], NB)

            def hidden_3(g):
                h = g[1] % 2
                act.wait_ge(c_arow[h], slot_count(g, 16))
                wait(act, c_r, count(g, U, -U))
                act.activation(ht[h][0:HID, :], arow[h][:, :], ACT.Relu, bias=rw1c[:, 1:2], scale=rw1c[:, 0:1]).then_inc(c_ht, 1)

            def features_3(g):
                h = g[1] % 2
                act.wait_ge(c_gat[h], slot_count(g, 16 * U))
                wait(act, c_fk, count(g, 1))
                vec = gat[h][:, 0, :, 8:32].rearrange("p t (v i) -> p t v i", i=3)
                act_copy(act, feat5[:, :, :, 0:3], vec)
                act_copy(act, feat5[:, :, :, 3:5], vec[:, :, :, 0:2])
                wait(act, c_use, count(g, U, -U))
                act_copy(act, fd[h][:, :, 0, :], gat[h][:, 0, :, 0:8])
                for i in range(3):
                    last = act_copy(act, fk[h][:, :, i, 0, :], vec[:, :, :, i])
                last.then_inc(c_feat, 1)

            def copy_3(g):
                h = g[1] % 2
                act.wait_ge(c_pay_p, count(g, 1, 1))
                for c in range(2):
                    wait(act, c_sc[c], landed_3((g[0], g[1] - 2), c))
                act_copy(act, pay1[h][:, :, :], psum[7][:, 0:U * D].rearrange("p (t f) -> p t f", t=U)).then_inc(c_pay, 1)

            def step_3(g, first=False):
                hidden_3(g)
                features_3(g)
                if not first:
                    copy_3((g[0], g[1] - 1))

            step_3((0, 0), first=True)
            step_3((0, 1))
            with act.Fori(0, NG // 2 - 1) as i:
                step_3((i, 2))
                step_3((i, 3))
            copy_3((0, NG - 1))

            def square_4(b):
                h = b[1] % 2
                act.wait_ge(z_y, count(b, 1, 1))
                wait(act, z_var, count(b, 1, -1))
                act.activation(wins(ld_c[h][:, :]), batch(b), ACT.Square, scale=D ** -0.5).then_inc(z_sq, 1)

            def root_4(b):
                act.wait_ge(z_var, count(b, 1, 1))
                act.activation(small(dev, b), small(var, b), ACT.Sqrt).then_inc(z_root, 1)

            staged(act, [square_4, None, root_4], NB)

        @block.tensor
        def _(pe):
            pe.wait_ge(s_const, 5)
            pe.wait_ge(s_erow, 1)
            for n in range(6):
                for c in range(2):
                    col = (n % 2) * NT + c * HALF
                    ins = pe.transpose(psum[n // 2][:, col:col + HALF], val_rows[:, n, c, :], ident[0:HALF, 0:HALF])
            ins.then_inc(s_ecol, 1)
            pe.wait_ge(s_ready, 1)
            pe.wait_ge(s_wld, N_WLD)

            def step_1(g):
                h = g[1] % 2
                pe.wait_ge(a_xw[h], slot_count(g, 16))
                wait(pe, a_xt, count(g, 2))
                for k in range(U):
                    ins = pe.transpose(two_banks(0)(k), xw[h][:, k, :], ident[:, :])
                ins.then_inc(a_xt_p, 1)
                pe.wait_ge(a_xt, count(g, 2, 2))
                wait(pe, a_xw1, count(g, 2))
                for k in range(U):
                    ins = pe.matmul(two_banks(4)(k), xt[:, k, :], w1c[:, :], start=True, stop=True)
                ins.then_inc(a_xw1_p, 1)
                pe.wait_ge(a_same, count(g, 2, 2))
                pe.wait_ge(a_wmsg, count(g, 1, 1))
                wait(pe, a_msg, count(g, 2))
                for k in range(U):
                    for c in range(2):
                        ins = pe.matmul(two_banks(2)(k)[D * c:D * c + D, :], wmsg[:, c, k, :], same[:, 1 - c, k, :],
                                        start=True, stop=True)
                ins.then_inc(a_msg_p, 1)
                pe.wait_ge(a_msg, count(g, 2, 2))
                wait(pe, a_pay, count(g, 1))
                for c in range(2):
                    for k in range(U):
                        ins = pe.matmul(psum[6 + c][:, D * k:D * k + D], msg_t[D * c:D * c + D, k, :],
                                        w1ab[D * c:D * c + D, :], start=True, stop=True)
                ins.then_inc(a_pay_p, 1)

            over_pairs(pe, step_1, NG)
            pe.wait_ge(a_xw1, 2 * NG)
            pe.wait_ge(a_pay, NG)
            pe.wait_ge(a_msg, 2 * NG)

            def turn(b):
                h = b[1] % 2
                pe.wait_ge(m_pre, count(b, 1, 1))
                wait(pe, m_act[0], count(b, 1))
                for w in range(BW):
                    ins = pe.transpose(psum[0][:, P * w:P * w + P], pre[h][:, P * w:P * w + P], ident[:, :])
                ins.then_inc(m_mm[0], 1)

            def layer(n, b):
                h = b[1] % 2
                pe.wait_ge(m_act[n - 1], count(b, 1, 1))
                wait(pe, m_act[n], count(b, 1))
                pe.matmul(psum[n][:, :], wl[n - 1][:, :], hid[n - 1][h][:, :], start=True, stop=True).then_inc(m_mm[n], 1)

            def back(b):
                h = b[1] % 2
                pe.wait_ge(m_act[3], count(b, 1, 1))
                wait(pe, m_y, count(b, 1))
                for w in range(BW):
                    ins = pe.matmul(psum[4][:, P * w:P * w + P], hid[3][h][:, P * w:P * w + P], centre[:, :],
                                    start=True, stop=True)
                ins.then_inc(m_mm[4], 1)

            staged(pe, [turn] + [lambda b, n=n: layer(n, b) for n in range(1, 4)] + [back], NB)
            pe.wait_ge(s_wprep, 1)
            for s in m_act:
                pe.wait_ge(s, NB)
            pe.wait_ge(m_y, NB)
            pe.wait_ge(c_ones, 2)

            def radial(g, k):
                h = g[1] % 2
                if k == 0:
                    pe.wait_ge(c_ht, count(g, 1, 1))
                wait(pe, c_use, count(g, U, k + 1 - U))
                pe.matmul(psum[k][:, 0:RC], ht[h][:, P * k:P * k + P], rw[:, :, :].rearrange("p a b -> p (a b)"),
                          start=True, stop=True).then_inc(c_r, 1)

            def sum_3(g):
                h = g[1] % 2
                pe.wait_ge(c_same, count(g, 1, 1))
                pe.wait_ge(c_msg, count(g, 1, 1))
                wait(pe, c_pay, count(g, 1))
                for k in range(U):
                    ins = pe.matmul(psum[7][:, D * k:D * k + D], same[:, h, k, :], msg1[h][:, k, :], start=True, stop=True)
                ins.then_inc(c_pay_p, 1)

            def step_3(g, first=False):
                for k in range(U):
                    radial(g, k)
                    if k == 2 and not first:
                        sum_3((g[0], g[1] - 1))

            step_3((0, 0), first=True)
            step_3((0, 1))
            with pe.Fori(0, NG // 2 - 1) as i:
                step_3((i, 2))
                step_3((i, 3))
            sum_3((0, NG - 1))

        @block.vector
        def _(dve):
            dve.memset(zeros[:, :], 0.0).then_inc(s_fill, 1)
            for t in (w1c, *wl):
                dve.memset(t[:, :], 0.0).then_inc(s_fill, 1)
            dve.memset(centre[:, :], 0.0).then_inc(s_fill, 1)
            dve.memset(key_i[:, :, NT:NT + 2 * U], 0).then_inc(s_fill, 1)
            dve.memset(sdst_all[:, NT:NT + U], 0).then_inc(s_fill, 1)
            dve.wait_ge(s_fill, 8)
            for j in range(J):
                s = slice(D * j, D * j + D)
                dve.memset(centre[s, s], -1.0 / D).then_inc(s_fill, 1)
            dve.wait_ge(s_fill, 12)
            dve.wait_ge(s_const, 5)
            dve.tensor_tensor(centred[:, :], centre[:, :], ident[:, :], ALU.add).then_inc(s_fill, 1)
            dve.wait_ge(s_fill, 13)
            dve.tensor_copy(centre[:, :], centred[:, :]).then_inc(s_fill, 1)
            dve.tensor_copy(tr_f[:, :], tr_i[:, :]).then_inc(s_fill, 1)

            dve.wait_ge(s_eld, 64)
            dve.tensor_copy(val_rows[:, 0:2], idx_rows[:, :, :, :])
            e3 = ea_rows[:, :, :].rearrange("r c (q i) -> r c q i", i=3)
            for n, i in enumerate((1, 2, 0)):
                ins = dve.tensor_copy(val_rows[:, 3 + n], e3[:, :, :, i])
            ins.then_inc(s_erow, 1)
            dve.wait_ge(s_ecol, 1)
            prep = Chain(dve, s_prep, 10)
            prep.begin((0, 0))
            keys = psum[0][:, 0:2 * NT].rearrange("p (c t) -> p c t", c=2)
            prep.mark(dve.tensor_copy(key_f[:, :, :], keys))
            prep.mark(dve.tensor_copy(key_i[:, :, 0:NT], keys))
            dve.wait_ge(s_fill, 15)
            prep.mark(dve.tensor_scalar(to_spare[:, :, :], keys, -1.0, tr_f[:, :], ALU.mult, ALU.add))
            prep.mark(dve.tensor_copy(w1e[:, :], psum[1][:, 0:NT]))
            prep.mark(dve.tensor_copy(rel[:, :, 0], psum[1][:, NT:2 * NT]))
            prep.mark(dve.tensor_copy(rel[:, :, 1:3], psum[2][:, 0:2 * NT].rearrange("p (c t) -> p t c", c=2)))
            prep.need()
            prep.mark(dve.tensor_tensor(relsq[:, :, :], rel[:, :, :], rel[:, :, :], ALU.mult))
            prep.need()
            dve.tensor_reduce(rsum[:, :], relsq[:, :, :], AX_X, ALU.add).then_inc(s_sum, 1)
            dve.wait_ge(s_norm, 1)
            prep.mark(dve.reciprocal(rinv[:, :], rnorm[:, :]))
            prep.need()
            prep.mark(dve.tensor_tensor(dir5[:, :, 0:3], rel[:, :, :], rinv[:, :].unsqueeze(2).broadcast_to([P, NT, 3]), ALU.mult))
            prep.need()
            prep.mark(dve.tensor_copy(dir5[:, :, 3:5], dir5[:, :, 0:2]))
            prep.end()
            prep.need()
            dve.tensor_copy(gidx[0][:, :, :], key_i[:, :, 0:U]).then_inc(a_idx, 1)
            dve.wait_ge(a_idx, 1)
            dve.memset(row_f[:, :, :], 0.0).then_inc(s_ready, 1)

            ch = Chain(dve, a_dve, 6)

            def step_1(g):
                h = g[1] % 2
                t0 = count(g, U)
                ts = bass.ds(t0, U)
                ch.begin(g)
                dve.wait_ge(a_rows[h], slot_count(g, 32))
                wait(dve, a_msg_p, count(g, 1))
                for c, rows in enumerate((rows_s[h], rows_d[h])):
                    dve.tensor_tensor(same[:, c], rows[:, :, :], key_f[:, c, ts].unsqueeze(2).broadcast_to([P, U, P]),
                                      ALU.is_equal).then_inc(a_same, 1)
                dve.wait_ge(a_same, count(g, 2, 2))
                for c in range(2):
                    ch.mark(dve.tensor_tensor(earlier[:, c], same[:, c], lower[:, :].unsqueeze(1).broadcast_to([P, U, P]), ALU.mult))
                ch.need()
                ch.mark(dve.tensor_reduce(dups[:, :, :], earlier[:, :, :, :], AX_X, ALU.add))
                ch.need()
                ch.mark(dve.scalar_tensor_tensor(out=spare_step[:, :, :], in0=dups[:, :, :], scalar=1.0,
                                                 in1=to_spare[:, :, ts], op0=ALU.min, op1=ALU.mult))
                ch.need()
                ch.mark(dve.tensor_tensor(row_f[:, :, :], spare_step[:, :, :], key_f[:, :, ts], ALU.add))
                ch.need()
                wait(dve, a_gat[1 - h], slot_count((g[0], g[1] - 1), 32 * U))
                dve.tensor_copy(gidx[1 - h][:, :, :], key_i[:, :, bass.ds(t0 + U, U)]).then_inc(a_idx, 1)
                dve.wait_ge(a_xw[h], slot_count(g, 16))
                xn = xw[h][:, :, :].rearrange("p w (j f) -> p (w j) f", f=D)
                ch.mark(dve.tensor_reduce(xmean[:, :], xn, AX_X, ALU.add))
                ch.need()
                wait(dve, a_xst[h], slot_count(g, 16) - 16)
                dve.scalar_tensor_tensor(out=xcen[h][:, :, :].rearrange("p w (j f) -> p (w j) f", f=D),
                                         in0=xmean[:, :].unsqueeze(2).broadcast_to([P, U * J, D]), scalar=-1.0 / D, in1=xn,
                                         op0=ALU.mult, op1=ALU.add).then_inc(a_xcen, 1)
                dve.wait_ge(a_gat[h], slot_count(g, 32 * U))
                dve.tensor_tensor(wmsg[:, :, :, :], gat[h][:, :, :, :],
                                  w1e[:, ts].unsqueeze(1).unsqueeze(3).broadcast_to([P, 2, U, D]), ALU.mult
                                  ).then_inc(a_wmsg, 1)
                for s in a_sc:
                    wait(dve, s, count(g, 16 * U, -16 * U))
                dve.tensor_copy(sdst_all[:, ts], row_f[:, 1, :])
                dve.tensor_copy(sidx[h][:, :, :], row_f[:, :, :]).then_inc(a_sidx, 1)
                ch.end()

            over_pairs(dve, step_1, NG)

            dve.wait_ge(s_wld, N_WLD)
            b = [rw_raw[:, 64 * n:64 * n + 64].rearrange("p (u v) -> p u v", v=8) for n in range(3)]
            b11 = rw_raw[:, 192:384].rearrange("p (u v k) -> p u v k", v=8, k=3)
            dve.tensor_scalar(rw[:, 0:8, 0:8], b[0], C_00, None, ALU.mult)
            dve.tensor_scalar(rw[:, 0:8, 8:16], b[1], C_00, None, ALU.mult)
            dve.tensor_scalar(rw[:, 8:16, 0:8], b[2], C_10, None, ALU.mult)
            dve.tensor_scalar(rw[:, 8:16, 8:16], b11[:, :, :, 2], C_11_2, None, ALU.mult)
            dve.tensor_scalar(rw[:, 16:24, 8:16], b11[:, :, :, 1], C_11_1, None, ALU.mult)
            dve.tensor_scalar(rw_t[:, :, :], b11[:, :, :, 2], -C_11_2 / 3.0, None, ALU.mult).then_inc(s_wchain, 1)
            dve.wait_ge(s_wchain, 1)
            dve.scalar_tensor_tensor(out=rw[:, 16:24, 0:8], in0=b11[:, :, :, 0], scalar=C_11_0, in1=rw_t[:, :, :],
                                     op0=ALU.mult, op1=ALU.add).then_inc(s_wprep, 1)

            def add_2(b):
                h = b[1] % 2
                dve.wait_ge(m_mm[4], count(b, 1, 1))
                dve.wait_ge(m_xc[h], slot_count(b, 16))
                dve.tensor_tensor(batch(b), wins(psum[4][:, :]), wins(ld_c[h][:, :]), ALU.add).then_inc(m_y, 1)

            mch = Chain(dve, m_dve, 11)

            def root_2(b):
                h = b[1] % 2
                mch.begin(b)
                dve.wait_ge(m_sq, count(b, 1, 1))
                dve.tensor_reduce(ssq[:, :], nodes(ysq[h][:, :]), AX_X, ALU.add).then_inc(m_ssq, 1)
                dve.wait_ge(m_ssq, count(b, 1, 1))
                v, y, t = vps[:, :], newton[0], newton[1]
                mch.mark(dve.tensor_scalar(v, ssq[:, :], EPS, None, ALU.add))
                mch.need()
                mch.mark(dve.tensor_scalar(y[:, :].bitcast(I32), v.bitcast(I32), -0.5, float(0x5f3759df), ALU.mult, ALU.add))
                for _ in range(3):
                    mch.need()
                    mch.mark(dve.tensor_tensor(t[:, :], y[:, :], y[:, :], ALU.mult))
                    mch.need()
                    mch.mark(dve.scalar_tensor_tensor(out=t[:, :], in0=t[:, :], scalar=-0.5, in1=v, op0=ALU.mult, op1=ALU.mult))
                    mch.need()
                    mch.mark(dve.scalar_tensor_tensor(out=y[:, :], in0=t[:, :], scalar=1.5, in1=y[:, :], op0=ALU.add, op1=ALU.mult))
                mch.need()
                dve.tensor_tensor(rows(b), rows(b), y[:, :].unsqueeze(2).broadcast_to([P, BW * J, D]), ALU.mult).then_inc(m_x1, 1)
                mch.end()

            staged(dve, [add_2, None, root_2], NB)

            for h in range(2):
                dve.memset(ht[h][HID:HID + 1, :], 1.0).then_inc(c_ones, 1)
            for h in range(2):
                dve.tensor_copy(gidx[h][:, 0, :], key_i[:, 0, U * h:U * h + U]).then_inc(c_gidx, 1)
            cch = Chain(dve, c_dve, 2)

            def reduce_3(g, k):
                q = k % 2
                dve.wait_ge(c_use, count(g, U, k + 1))
                dve.tensor_reduce(red_s[:, k, :], prod_s[q][:, :, :], AX_X, ALU.add)
                dve.tensor_reduce(red_v[:, k, :, :], prod_v[q][:, :, :, :], AX_X, ALU.add).then_inc(c_red, 1)

            def step_3(g):
                h = g[1] % 2
                t0 = count(g, U)
                ts = bass.ds(t0, U)
                cch.begin(g)
                dve.wait_ge(c_rows[h], slot_count(g, 16))
                wait(dve, c_pay_p, count(g, 1, -1))
                dve.tensor_tensor(same[:, h], rows_d[h][:, :, :], key_f[:, 1, ts].unsqueeze(2).broadcast_to([P, U, P]),
                                  ALU.is_equal).then_inc(c_same, 1)
                dve.wait_ge(c_feat, count(g, 1, 1))
                dve.tensor_copy(gidx[h][:, 0, :], key_i[:, 0, bass.ds(t0 + 2 * U, U)]).then_inc(c_gidx, 1)

                def along(a):
                    return dir5[:, ts, a:a + 3].unsqueeze(2).broadcast_to([P, U, 8, 3])

                dve.tensor_tensor(dprod[:, :, :, :], feat5[:, :, :, 0:3], along(0), ALU.mult)
                dve.tensor_tensor(kp[:, 0], feat5[:, :, :, 2:5], along(1), ALU.mult)
                cch.mark(dve.tensor_tensor(kp[:, 1], feat5[:, :, :, 1:4], along(2), ALU.mult))
                cch.need()
                dve.tensor_reduce(fd[h][:, :, 1, :], dprod[:, :, :, :], AX_X, ALU.add)
                dve.tensor_tensor(fk[h][:, :, :, 1, :].rearrange("p t i v -> p t v i"), kp[:, 0], kp[:, 1],
                                  ALU.subtract).then_inc(c_fk, 1)
                dve.wait_ge(c_fk, count(g, 1, 1))
                for k in range(U):
                    q = k % 2
                    dve.wait_ge(c_r, count(g, U, k + 1))
                    wait(dve, c_red, count(g, U, max(k - 1, 0)))
                    r_s = psum[k][:, 0:256].rearrange("p (u v) -> p u v", v=16)
                    r_v = psum[k][:, 256:384].rearrange("p (u v) -> p u v", v=16)
                    dve.tensor_tensor(prod_s[q][:, :, :], r_s, fd[h][:, k].rearrange("p a v -> p (a v)").unsqueeze(1).broadcast_to([P, 16, 16]),
                                      ALU.mult)
                    dve.tensor_tensor(prod_v[q][:, :, :, :], r_v.unsqueeze(2).broadcast_to([P, 8, 3, 16]),
                                      fk[h][:, k].rearrange("p i a v -> p i (a v)").unsqueeze(1).broadcast_to([P, 8, 3, 16]),
                                      ALU.mult).then_inc(c_use, 1)
                    if k >= 1:
                        reduce_3(g, k - 1)
                reduce_3(g, U - 1)
                dve.wait_ge(c_red, count(g, U, U))
                cch.mark(dve.tensor_tensor(rq[:, :, :, :], red_s[:, :, 8:16].unsqueeze(3).broadcast_to([P, U, 8, 3]), along(0), ALU.mult))
                cch.need()
                dve.tensor_copy(msg1[h][:, :, 0:8], red_s[:, :, 0:8])
                dve.tensor_tensor(msg1[h][:, :, 8:32].rearrange("p t (u i) -> p t u i", i=3), rq[:, :, :, :], red_v[:, :, :, :],
                                  ALU.add).then_inc(c_msg, 1)
                for c in range(2):
                    wait(dve, c_sc[c], landed_3((g[0], g[1] - 2), c))
                dve.tensor_copy(sidx[h][:, 0, :], sdst_all[:, ts]).then_inc(c_sidx, 1)
                cch.end()

            over_pairs(dve, step_3, NG)

            zch = Chain(dve, z_dve, 2)

            def add_4(b):
                h = b[1] % 2
                zch.begin(b)
                dve.wait_ge(z_sum, count(b, 1, 1))
                zch.mark(dve.tensor_tensor(wins(pre[h][:, :]), wins(pre[h][:, :]), batch(b), ALU.add))
                zch.need()
                zch.mark(dve.tensor_reduce(ssq[:, :], nodes(pre[h][:, :]), AX_X, ALU.add))
                zch.need()
                dve.scalar_tensor_tensor(out=rows(b), in0=ssq[:, :].unsqueeze(2).broadcast_to([P, BW * J, D]),
                                         scalar=-1.0 / D, in1=nodes(pre[h][:, :]), op0=ALU.mult, op1=ALU.add).then_inc(z_y, 1)
                zch.end()

            def var_4(b):
                h = b[1] % 2
                dve.wait_ge(z_sq, count(b, 1, 1))
                wait(dve, z_var, count(b, 1))
                dve.tensor_reduce(rstd[:, :], nodes(ld_c[h][:, :]), AX_X, ALU.add).then_inc(z_n, 1)
                dve.wait_ge(z_n, count(b, 1, 1))
                dve.tensor_scalar(small(var, b), rstd[:, :], EPS, None, ALU.add).then_inc(z_var, 1)

            def inverse_4(b):
                dve.wait_ge(z_root, count(b, 1, 1))
                dve.reciprocal(small(rsd, b), small(dev, b)).then_inc(z_r, 1)

            staged(dve, [add_4, None, var_4, None, inverse_4], NB)


_INS = ["x", "src", "dst", "edge_attr_3", "edge_weight", "edge_weight1",
        "L0_gnn_W1", "L0_gnn_b1", "L0_gnn_W2", "L0_gnn_b2", "L0_gnn_W3", "L0_gnn_b3", "L0_gnn_W4", "L0_gnn_b4",
        "L1_gnn_w1", "L1_gnn_b1", "L1_gnn_w2", "L1_gnn_b2"]


def kernel(**inputs):
    import numpy as np
    import concourse.bacc as bacc
    from concourse.bass_utils import run_bass_kernel_spmd

    a = {n: np.asarray(inputs[n]) for n in _INS}
    more = NT * P - E
    a["x"] = np.concatenate([a["x"], np.zeros((NPAD - N, D), a["x"].dtype)])
    spare = np.arange(PAD_NODE, PAD_NODE + more)
    for n in ("src", "dst"):
        a[n] = np.concatenate([a[n], spare.astype(a[n].dtype)]).reshape(NT, P)
    a["edge_attr_3"] = np.concatenate([a["edge_attr_3"], np.ones((more, 3), a["edge_attr_3"].dtype)]).reshape(NT, P * 3)
    for n in ("edge_weight", "edge_weight1"):
        v = a[n].reshape(-1)
        a[n] = np.concatenate([v, np.zeros(more, v.dtype)]).reshape(NT, P)
    for n in ("L0_gnn_b1", "L0_gnn_b2", "L0_gnn_b3", "L0_gnn_b4", "L1_gnn_b1"):
        a[n] = a[n].reshape(-1, 1)
    a["L1_gnn_w1"] = a["L1_gnn_w1"].reshape(-1, 1)
    a["L1_gnn_b2"] = a["L1_gnn_b2"].reshape(1, -1)

    nc = bacc.Bacc("TRN2", target_bir_lowering=False, num_devices=1)
    arrays, args = {}, []
    for n in _INS:
        v = np.ascontiguousarray(a[n])
        arrays[f"in_{n}"] = v
        args.append(nc.dram_tensor(f"in_{n}", v.shape, mybir.dt.from_np(v.dtype), kind="ExternalInput").ap())
    out = nc.dram_tensor("out", (NPAD, D), F32, kind="ExternalOutput").ap()
    gnn_kernel(nc, *args, out)
    r = run_bass_kernel_spmd(nc, [arrays], core_ids=[0])
    return r.results[0]["out"][:N]
```

```python
from contextlib import ExitStack
from math import sqrt

import concourse.bass as bass
from concourse import mybir

F32 = mybir.dt.float32
I32 = mybir.dt.int32
ALU = mybir.AluOpType
ACT = mybir.ActivationFunctionType
AX_X = mybir.AxisListType.X

P = 128
N, E, D = 100000, 25000, 32
J = 4
WIN = P * J
NW = -(-N // WIN)
NPAD = NW * WIN
NT = -(-E // P)
U = 7
NG = NT // U
HALF = NT // 2
BW = 4
NB = NW // BW
BC = BW * P
PAD_NODE = N + P
EPS = 1e-5
LEAD = NG // 2
AHEAD = 4
HID, RC = 64, 384
assert NT == NW and NG * U == NT and NG % 4 == 0 and LEAD % 2 == 0 and NB * BW == NW and NB % 2 == 1
assert PAD_NODE + NT * P - E <= NPAD

C_00 = 0.25
C_10 = sqrt(3.0 / 32.0)
C_11_0 = sqrt(1.0 / 32.0)
C_11_1 = sqrt(3.0 / 64.0)
C_11_2 = 0.375


def count(g, per, off=0):
    i, k = g
    return i * (2 * per) + (k * per + off)


def slot_count(g, per):
    i, k = g
    return i * per + (k // 2 + 1) * per


def wait(eng, sem, value):
    if isinstance(value, int) and value <= 0:
        return
    eng.wait_ge(sem, value)


def over_pairs(eng, step, n):
    step((0, 0))
    step((0, 1))
    with eng.Fori(0, n // 2 - 1) as i:
        step((i, 2))
        step((i, 3))
    if n % 2:
        step((n // 2 - 1, 2))


def led(eng, part_a, part_b):
    def both(g):
        part_b(g)
        part_a((g[0], g[1] + LEAD))

    over_pairs(eng, part_a, LEAD)
    over_pairs(eng, both, NG - LEAD)
    with eng.Fori(0, LEAD // 2) as i:
        part_b((i, NG - LEAD))
        part_b((i, NG - LEAD + 1))


def staged(eng, stages, n, head=None):
    lag = len(stages)

    def step(s, ends=False):
        if head and (not ends or s[1] < n):
            head(s)
        for k in reversed(range(lag)):
            if stages[k] and (not ends or 0 <= s[1] - k < n):
                stages[k]((s[0], s[1] - k))

    peeled = lag + 1 + (lag + 1) % 2
    pairs = (n - peeled) // 2
    for s in range(peeled):
        step((0, s), ends=True)
    with eng.Fori(0, pairs) as i:
        step((i, peeled))
        step((i, peeled + 1))
    for s in range(peeled + 2 * pairs, n + lag - 1):
        step((0, s), ends=True)


def act_copy(act, out, in_):
    return act.activation(out, in_, ACT.Copy)


def wait_here(eng, sem, value, passed):
    if isinstance(value, int):
        return wait(eng, sem, value)
    eng.wait_ge(sem, value)
    eng.sem_inc(passed, 1)


class Chain:

    def __init__(self, eng, sem, per, two_steps=False):
        self.eng, self.sem, self.per, self.two_steps = eng, sem, per, two_steps

    def begin(self, g):
        self.g, self.n = g, 0

    def mark(self, instruction):
        instruction.then_inc(self.sem, 1)
        self.n += 1

    def need(self, back=0):
        before = slot_count(self.g, self.per) - self.per if self.two_steps else count(self.g, self.per)
        wait(self.eng, self.sem, before + (self.n - back))

    def end(self):
        assert self.n == self.per, (self.n, self.per)


def gnn_kernel(nc, x, src, dst, ea, ew, ew1, W1, b1, W2, b2, W3, b3, W4, b4, rw1, rb1, rw2, rb2, out):
    x_w = x.rearrange("(w p j) f -> p w (j f)", p=P, j=J)
    out_w = out.rearrange("(w p j) f -> p w (j f)", p=P, j=J)

    def dram(name):
        return nc.dram_tensor(name, (NPAD, D), F32, kind="Internal").ap()

    def windows(a):
        return a.rearrange("(w p j) f -> p w (j f)", p=P, j=J)

    acc_in, acc_out, xc_d, x1_d = dram("acc_in"), dram("acc_out"), dram("xc_d"), dram("x1_d")
    acc_l1 = [dram("acc_l1a"), dram("acc_l1b")]

    with ExitStack() as ctx:
        def sb(name, shape, dt=F32):
            return ctx.enter_context(nc.sbuf_tensor(name, shape, dt))

        edge_prep, phase_1, phase_2 = ExitStack(), ExitStack(), ExitStack()

        def sb0(name, shape, dt=F32):
            return edge_prep.enter_context(nc.sbuf_tensor(name, shape, dt))

        def sb1(name, shape, dt=F32):
            return phase_1.enter_context(nc.sbuf_tensor(name, shape, dt))

        def sb2(name, shape, dt=F32):
            return phase_2.enter_context(nc.sbuf_tensor(name, shape, dt))

        def sem(name):
            return ctx.enter_context(nc.semaphore(name))

        def pair(make, name, *a):
            return [make(f"{name}{h}", *a) for h in range(2)]

        res = sb("res", [P, NW, P])
        ident = sb("ident", [P, P])
        lower = sb("lower", [P, P])
        zeros = sb("zeros", [P, 512])
        tr_i = sb("tr_i", [P, 1], I32)
        tr_f = sb("tr_f", [P, 1])
        key_f = sb("key_f", [P, 2, NT])
        key_i = sb("key_i", [P, 2, NT + 2 * U], I32)
        to_spare = sb("to_spare", [P, 2, NT])
        w1e = sb("w1e", [P, NT])
        dir5 = sb("dir5", [P, NT, 5])
        sdst_all = sb("sdst_all", [P, NT + U], I32)
        w1ab = sb("w1ab", [D, 2, D])
        w1c = sb("w1c", [P, P])
        wl = [sb(f"wl{n}", [P, P]) for n in range(3)]
        centre = sb("centre", [P, P])
        centred = sb("centred", [P, P])
        bias = sb("bias", [P, 4])
        eps = sb("eps", [P, 1])
        rw1c = sb("rw1c", [HID, 2])
        rw_raw = sb("rw_raw", [HID + 1, RC])
        rw = sb("rw", [HID + 1, 24, 16])
        rw_t = sb("rw_t", [HID + 1, 8, 8])

        rows_d = pair(sb, "rows_d", [P, U, P], I32)
        gidx = pair(sb, "gidx", [P, U], I32)
        sidx = pair(sb, "sidx", [P, 2, U], I32)
        gidx_b = pair(sb, "gidx_b", [P, U], I32)
        gat = pair(sb, "gat", [P, U, D])
        same = sb("same", [P, 2, U, P])

        idx_rows = sb0("idx_rows", [HALF, 2, 2, P], I32)
        val_rows = sb0("val_rows", [HALF, 6, 2, P])
        ea_rows = sb0("ea_rows", [HALF, 2, P * 3])
        rel = sb0("rel", [P, NT, 3])
        relsq = sb0("relsq", [P, NT, 3])
        rnorm = sb0("rnorm", [P, NT])
        rsum = sb0("rsum", [P, NT])
        rinv = sb0("rinv", [P, NT])
        edge_prep.close()

        pay_in = sb1("pay_in", [P, NT, D])
        rows_s = pair(sb1, "rows_s", [P, U, P], I32)
        gat_b = pair(sb1, "gat_b", [P, U, D])
        wmsg = sb1("wmsg", [P, 2, U, D])
        earlier = sb1("earlier", [P, U, P])
        dups = sb1("dups", [P, 2, U])
        spare_step = sb1("spare_step", [P, 2, U])
        row_f = sb1("row_f", [P, 2, U])
        msg_t = sb1("msg_t", [D, 2, U, P])
        pay = pair(sb1, "pay", [P, 2, U, D])
        xw = pair(sb1, "xw", [P, U, P])
        xt = sb1("xt", [P, U, P])
        xmean = sb1("xmean", [P, U * J])
        xcen = pair(sb1, "xcen", [P, U, P])
        phase_1.close()

        ld_a = pair(sb, "ld_a", [P, BC])
        ld_b = pair(sb, "ld_b", [P, BC])
        ld_c = pair(sb, "ld_c", [P, BC])
        pre = pair(sb, "pre", [P, BC])
        ysq = pair(sb, "ysq", [P, BC])
        ssq = sb("ssq", [P, BW * J])
        vps = sb("vps", [P, 2 * BW * J])
        ssq_2 = sb("ssq_2", [P, 2, BW * J])
        var = sb("var", [P, NB, BW * J])
        dev = sb("dev", [P, NB, BW * J])
        rsd = sb("rsd", [P, NB, BW * J])
        newton = pair(sb, "newton", [P, 2 * BW * J])

        hid = [pair(sb2, f"hid{n}_", [P, BC]) for n in range(4)]
        phase_2.close()

        arow = pair(sb, "arow", [HID, U * P])
        ht = pair(sb, "ht", [HID + 1, U * P])
        feat5 = sb("feat5", [P, U, 8, 5])
        fd = pair(sb, "fd", [P, U, 2, 8])
        fk = pair(sb, "fk", [P, U, 3, 2, 8])
        dprod = sb("dprod", [P, U, 8, 3])
        kp = sb("kp", [P, 2, U, 8, 3])
        prod_s = [sb(f"prod_s{n}", [P, 16, 16]) for n in range(3)]
        prod_v = [sb(f"prod_v{n}", [P, 8, 3, 16]) for n in range(3)]
        red_s = sb("red_s", [P, U, 16])
        red_v = sb("red_v", [P, U, 8, 3])
        rq = sb("rq", [P, U, 8, 3])
        msg1 = pair(sb, "msg1", [P, U, D])
        pay1 = pair(sb, "pay1", [P, U, D])

        psum = [ctx.enter_context(nc.psum_tensor(f"bank{n}", [P, 512], F32)) for n in range(8)]

        def two_banks(n):
            return lambda k: psum[n + k // 4][:, (k % 4) * P:(k % 4 + 1) * P]

        bank_2 = [(psum[0], psum[5]), (psum[1], psum[7]), (psum[2],) * 2, (psum[3],) * 2, (psum[4], psum[6])]
        held_2 = [-1, -1, 0, 0, -1]

        s_const = sem("s_const")
        s_fill = sem("s_fill")
        s_wld = sem("s_wld")
        s_eld = sem("s_eld")
        s_zero = sem("s_zero")
        s_zero1 = sem("s_zero1")
        s_erow = sem("s_erow")
        s_ecol = sem("s_ecol")
        s_prep = sem("s_prep")
        s_passed = sem("s_passed")
        s_spaced = sem("s_spaced")
        s_sum = sem("s_sum")
        s_norm = sem("s_norm")
        s_ready = sem("s_ready")
        s_wchain = sem("s_wchain")
        s_wprep = sem("s_wprep")

        block = ctx.enter_context(nc.Block())

        a_rows = pair(sem, "a_rows")
        a_idx = sem("a_idx")
        a_gat = pair(sem, "a_gat")
        a_same = sem("a_same")
        a_wmsg = sem("a_wmsg")
        a_dve = sem("a_dve")
        a_msg_p = sem("a_msg_p")
        a_pay_p = sem("a_pay_p")
        a_msg = sem("a_msg")
        a_pay = sem("a_pay")

        b_rows = pair(sem, "b_rows")
        b_xw = pair(sem, "b_xwin")
        b_xst = pair(sem, "b_xst")
        b_idx = sem("b_idx")
        b_gat = pair(sem, "b_gat")
        b_same = sem("b_same")
        b_sidx = sem("b_sidx")
        b_xcen = sem("b_xcen")
        b_wmsg = sem("b_wmsg")
        b_dve = sem("b_dve")
        b_xt_p = sem("b_xt_p")
        b_msg_p = sem("b_msg_p")
        b_xw1_p = sem("b_xw1_p")
        b_pay_p = sem("b_pay_p")
        b_xt = sem("b_xt")
        b_msg = sem("b_msg")
        b_xw1 = sem("b_xw1")
        b_pay = sem("b_pay")
        b_sc = [sem("b_sc_in"), sem("b_sc_out")]

        m_ld = pair(sem, "m_ld")
        m_xc = pair(sem, "m_xc")
        m_sum1 = sem("m_sum1")
        m_pre = sem("m_pre")
        m_mm = [sem(f"m_mm{n}") for n in range(5)]
        m_act = [sem(f"m_act{n}") for n in range(4)]
        m_y = sem("m_y")
        m_sq = sem("m_sq")
        m_ssq = sem("m_ssq")
        m_dve = sem("m_dve")
        m_x1 = sem("m_x1")
        m_st = sem("m_st")

        c_rows = pair(sem, "c_rows")
        c_arow = pair(sem, "c_arow")
        c_ones = sem("c_ones")
        c_gidx = sem("c_gidx")
        c_sidx = sem("c_sidx")
        c_red = sem("c_red")
        c_gat = pair(sem, "c_gat")
        c_same = sem("c_same")
        c_dve = sem("c_dve")
        c_feat = sem("c_feat")
        c_fk = sem("c_fk")
        c_ht = sem("c_ht")
        c_r = sem("c_r")
        c_use = sem("c_use")
        c_msg = sem("c_msg")
        c_pay_p = sem("c_pay_p")
        c_pay = sem("c_pay")
        c_sc = [sem("c_sc_a"), sem("c_sc_b")]

        z_ld = pair(sem, "z_ld")
        z_n = sem("z_n")
        z_sum = sem("z_sum")
        z_y = sem("z_y")
        z_sq = sem("z_sq")
        z_var = sem("z_var")
        z_root = sem("z_root")
        z_r = sem("z_r")
        z_out = sem("z_out")
        z_st = pair(sem, "z_st")

        def wins(a):
            return a.rearrange("p (w c) -> p w c", w=BW)

        def nodes(a):
            return a.rearrange("p (n f) -> p n f", f=D)

        def batch(b):
            return res[:, bass.ds(count(b, BW), BW), :]

        def rows(b):
            return batch(b).rearrange("p w (j f) -> p (w j) f", f=D)

        def small(a, b):
            return a[:, bass.ds(count(b, 1), 1), :].rearrange("p o n -> p (o n)")

        def landed_3(g, c, more=0):
            i, k = g
            in_pair = [(h + t) % 2 for h in range(k % 2 + 1) for t in range(U)].count(c)
            return i * (16 * U) + 16 * ((k // 2) * U + in_pair + more)

        N_WLD = 16 * (8 * J + 6)

        @block.sync
        def _(sp):
            half = lambda a: a.rearrange("(c r) q -> r c q", c=2)
            sp.dma_start(idx_rows[:, 0], half(src)).then_inc(s_eld, 16)
            sp.dma_start(idx_rows[:, 1], half(dst)).then_inc(s_eld, 16)
            sp.dma_start(val_rows[:, 2], half(ew1)).then_inc(s_eld, 16)
            sp.dma_start(ea_rows[:, :, :], half(ea)).then_inc(s_eld, 16)
            sp.wait_ge(s_fill, 6)

            def clear_slice(n):
                for a in (acc_in, acc_out):
                    sp.dma_start(windows(a)[:, bass.ds(n, 2 * U), :],
                                 zeros[:, 0:P].unsqueeze(1).broadcast_to([P, 2 * U, P])).then_inc(s_zero, 16)

            def load_a(g):
                h = g[1] % 2
                wait(sp, a_same, count(g, 1, -1))
                sp.dma_start(rows_d[h][:, :, :], dst[bass.ds(count(g, U), U), :].partition_broadcast(P)).then_inc(a_rows[h], 16)

            def spaced(g, k):
                wait_here(sp, b_sc[0], count(g, 16 * U, 16 * (k - 3 * U)), s_spaced)

            def load_b(g):
                h = g[1] % 2
                t0 = count(g, U)
                spaced(g, 5)
                wait(sp, b_same, count(g, 1, -1))
                sp.dma_start(rows_s[h][:, :, :], src[bass.ds(t0, U), :].partition_broadcast(P)).then_inc(b_rows[h], 16)
                spaced(g, 6)
                wait(sp, b_xt_p, count(g, 1, -1))
                wait(sp, b_xcen, count(g, 1, -1))
                sp.dma_start(xw[h][:, :, :], x_w[:, bass.ds(t0, U), :]).then_inc(b_xw[h], 16)

            for n, wt in enumerate((W1[2 * D:3 * D, :], W2, W3, W4)):
                for j in range(J):
                    s = slice(D * j, D * j + D)
                    sp.dma_start((w1c, *wl)[n][s, s], wt).then_inc(s_wld, 16)
            for n, b in enumerate((b1, b2, b3, b4)):
                for j in range(J):
                    sp.dma_start(bias[D * j:D * j + D, n:n + 1], b).then_inc(s_wld, 16)
            for c in range(2):
                sp.dma_start(w1ab[:, c, :], W1[D * c:D * c + D, :]).then_inc(s_wld, 16)
            sp.dma_start(rw1c[:, 0:1], rw1).then_inc(s_wld, 16)
            sp.dma_start(rw1c[:, 1:2], rb1).then_inc(s_wld, 16)
            sp.dma_start(rw_raw[0:HID, :], rw2).then_inc(s_wld, 16)
            sp.dma_start(rw_raw[HID:HID + 1, :], rb2).then_inc(s_wld, 16)

            def lead(g):
                load_a(g)
                clear_slice(count(g, 2 * U))

            over_pairs(sp, lead, LEAD)

            def store_b(g):
                h = g[1] % 2
                spaced((g[0], g[1] + 2), 2)
                sp.wait_ge(b_xcen, count(g, 1, 1))
                sp.dma_start(windows(xc_d)[:, bass.ds(count(g, U), U), :], xcen[h][:, :, :]).then_inc(b_xst[h], 16)

            def clear_b(g):
                spaced((g[0], g[1] + 2), 3)
                sp.dma_start(windows(acc_l1[1])[:, bass.ds(count(g, U), U), :],
                             zeros[:, 0:P].unsqueeze(1).broadcast_to([P, U, P])).then_inc(s_zero1, 16)

            def both(g):
                spaced((g[0], g[1] + 1), 4)
                load_a((g[0], g[1] + LEAD))
                load_b((g[0], g[1] + 1))
                store_b(g)
                clear_b(g)

            load_b((0, 0))
            both((0, 0))
            both((0, 1))
            with sp.Fori(0, (NG - LEAD) // 2 - 1) as i:
                both((i, 2))
                both((i, 3))

            def tail(g):
                load_b((g[0], g[1] + 1))
                store_b(g)
                clear_b(g)

            with sp.Fori(0, LEAD // 2 - 1) as i:
                tail((i, NG - LEAD))
                tail((i, NG - LEAD + 1))
            tail((0, NG - 2))
            store_b((0, NG - 1))
            clear_b((0, NG - 1))
            for h in range(2):
                sp.wait_ge(b_xst[h], 16 * NG // 2)
            for s in b_sc:
                sp.wait_ge(s, 16 * NT)

            def load_2(b):
                h = b[1] % 2
                ws = bass.ds(count(b, BW), BW)
                wait(sp, m_pre, count(b, 1, -1))
                for buf, a in ((ld_a[h], acc_in), (ld_b[h], acc_out)):
                    sp.dma_start(buf[:, :].rearrange("p (w c) -> p w c", w=BW), windows(a)[:, ws, :]).then_inc(m_ld[h], 16)

            def load_xc_2(b):
                h = b[1] % 2
                ws = bass.ds(count(b, BW), BW)
                wait(sp, m_y, count(b, 1, -1))
                sp.dma_start(ld_c[h][:, :].rearrange("p (w c) -> p w c", w=BW), windows(xc_d)[:, ws, :]).then_inc(m_xc[h], 16)

            def store_2(b):
                ws = bass.ds(count(b, BW), BW)
                sp.wait_ge(m_x1, count(b, 1, 1))
                for a in (x1_d, acc_l1[0]):
                    sp.dma_start(windows(a)[:, ws, :], res[:, ws, :]).then_inc(m_st, 16)

            staged(sp, [load_2, None, None, None, None, load_xc_2] + [None] * 5 + [store_2], NB)

            def load_3(g):
                h = g[1] % 2
                t0 = count(g, U)
                wait(sp, c_same, count(g, 1, -1))
                sp.dma_start(rows_d[h][:, :, :], dst[bass.ds(t0, U), :].partition_broadcast(P)).then_inc(c_rows[h], 16)
                wait(sp, c_ht, count(g, 1, -1))
                sp.dma_start(arow[h][:, :].rearrange("p (t q) -> p t q", t=U),
                             ew[bass.ds(t0, U), :].partition_broadcast(HID)).then_inc(c_arow[h], 16)

            over_pairs(sp, load_3, NG)
            for s in c_sc:
                sp.wait_ge(s, 16 * NT // 2)

            def load_4(b):
                h = b[1] % 2
                wait(sp, z_sum, count(b, 1, -1))
                for buf, a in ((ld_a[h], acc_l1[0]), (ld_b[h], acc_l1[1])):
                    sp.dma_start(buf[:, :].rearrange("p (w c) -> p w c", w=BW),
                                 windows(a)[:, bass.ds(count(b, BW), BW), :]).then_inc(z_ld[h], 16)

            def store_4(b):
                h = b[1] % 2
                sp.wait_ge(z_out, count(b, 1, 1))
                sp.dma_start(out_w[:, bass.ds(count(b, BW), BW), :],
                             ysq[h][:, :].rearrange("p (w c) -> p w c", w=BW)).then_inc(z_st[h], 16)

            staged(sp, [load_4] + [None] * 7 + [store_4], NB)
            sp.wait_ge(z_st[0], 16 * (NB // 2 + 1))
            sp.wait_ge(z_st[1], 16 * (NB // 2))

        @block.gpsimd
        def _(pool):
            pool.memset(ident[:, :], 0.0).then_inc(s_const, 1)
            pool.memset(lower[:, :], 1.0).then_inc(s_const, 1)
            pool.iota(tr_i[:, :], [[0, 1]], base=N, channel_multiplier=1).then_inc(s_const, 1)
            pool.wait_ge(s_const, 3)
            pool.affine_select(out=ident[:, :], in_=ident[:, :], compare_op=ALU.not_equal, fill=1.0, base=0,
                               pattern=[[-1, P]], channel_multiplier=1).then_inc(s_const, 1)
            pool.affine_select(out=lower[:, :], in_=lower[:, :], compare_op=ALU.is_gt, fill=0.0, base=0,
                               pattern=[[-1, P]], channel_multiplier=1).then_inc(s_const, 1)

            def gather(rows, k, table, idx, sem_):
                pool.indirect_dma_start(rows[:, k, :], None, table,
                                        bass.IndirectOffsetOnAxis(ap=idx[:, k:k + 1], axis=0)).then_inc(sem_, 16)

            def ready_a(g):
                wait_here(pool, a_idx, count(g, 1, 1), s_passed)
                wait_here(pool, a_wmsg, count(g, 1, -1), s_passed)

            def gather_a(g, k):
                h = g[1] % 2
                gather(gat[h], k, x, gidx[h], a_gat[h])

            def lead(g):
                ready_a(g)
                for k in range(U):
                    gather_a(g, k)

            over_pairs(pool, lead, LEAD)

            def scatter_b(g, c, k):
                h = g[1] % 2
                wait_here(pool, b_sc[c], count(g, 16 * U, 16 * k), s_passed)
                pool.indirect_dma_start((acc_in, acc_out)[c], bass.IndirectOffsetOnAxis(ap=sidx[h][:, c, k:k + 1], axis=0),
                                        pay[h][:, c, k, :], None, compute_op=ALU.add).then_inc(b_sc[c], 16)

            def ready_b(g):
                wait_here(pool, b_pay, count(g, 1, 1), s_passed)
                wait_here(pool, b_sidx, count(g, 1, 1), s_passed)

            def step_b(g, first=False, with_a=True):
                h = g[1] % 2
                before, ahead = (g[0], g[1] - 2), (g[0], g[1] + LEAD)
                wait_here(pool, b_idx, count(g, 1, 1), s_passed)
                wait_here(pool, b_wmsg, count(g, 1, -1), s_passed)
                if with_a:
                    ready_a(ahead)
                for k in range(U):
                    gather(gat_b[h], k, x, gidx_b[h], b_gat[h])
                    if not first:
                        if k == 0:
                            ready_b(before)
                        scatter_b(before, 0, k)
                    if with_a:
                        gather_a(ahead, k)
                    if not first:
                        scatter_b(before, 1, k)

            step_b((0, 0), first=True)
            step_b((0, 1), first=True)
            pool.wait_ge(s_zero, 16 * 2 * (NW // (2 * U)))
            step_b((0, 2))
            step_b((0, 3))
            with pool.Fori(0, (NG - LEAD) // 2 - 2) as i:
                step_b((i, 4))
                step_b((i, 5))
            with pool.Fori(0, LEAD // 2) as i:
                step_b((i, NG - LEAD), with_a=False)
                step_b((i, NG - LEAD + 1), with_a=False)
            for g in (NG - 2, NG - 1):
                ready_b((0, g))
                for k in range(U):
                    scatter_b((0, g), 0, k)
                    scatter_b((0, g), 1, k)
            for s in b_sc:
                pool.wait_ge(s, 16 * NT)

            pool.wait_ge(b_xw1, 2 * NG)

            def step_2(b):
                h = b[1] % 2
                pool.wait_ge(m_ld[h], slot_count(b, 32))
                wait(pool, m_mm[0], count(b, 1, -1))
                pool.tensor_tensor(ld_a[h][:, :], ld_a[h][:, :], ld_b[h][:, :], ALU.add).then_inc(m_sum1, 1)
                pool.wait_ge(m_sum1, count(b, 1, 1))
                pool.tensor_tensor(pre[h][:, :].rearrange("p (w c) -> p w c", w=BW), ld_a[h][:, :].rearrange("p (w c) -> p w c", w=BW),
                                   res[:, bass.ds(count(b, BW), BW), :], ALU.add).then_inc(m_pre, 1)

            over_pairs(pool, step_2, NB)

            def scatter_3(g, k):
                h = g[1] % 2
                c = (h + k) % 2
                earlier_3 = [(h + a) % 2 for a in range(k)].count(c)
                wait_here(pool, c_sc[c], landed_3((g[0], g[1] - 1), c, earlier_3), s_passed)
                pool.indirect_dma_start(acc_l1[c], bass.IndirectOffsetOnAxis(ap=sidx[h][:, 0, k:k + 1], axis=0),
                                        pay1[h][:, k, :], None, compute_op=ALU.add).then_inc(c_sc[c], 16)

            def step_3(g):
                h = g[1] % 2
                wait_here(pool, c_gidx, count(g, 1, 1), s_passed)
                wait_here(pool, c_fk, count(g, 1, -1), s_passed)
                for k in range(U):
                    gather(gat[h], k, x1_d, gidx[h], c_gat[h])
                    if k < AHEAD:
                        if g[1] >= 3:
                            scatter_3((g[0], g[1] - 3), U - AHEAD + k)
                    elif g[1] >= 2:
                        if k == AHEAD:
                            ready_3((g[0], g[1] - 2))
                        scatter_3((g[0], g[1] - 2), k - AHEAD)

            def ready_3(g):
                wait_here(pool, c_pay, count(g, 1, 1), s_passed)
                wait_here(pool, c_sidx, count(g, 1, 1), s_passed)

            pool.wait_ge(m_st, 16 * 2 * NB)
            pool.wait_ge(s_zero1, 16 * NG)
            for k in range(4):
                step_3((0, k))
            with pool.Fori(0, NG // 2 - 2) as i:
                step_3((i, 4))
                step_3((i, 5))
            for k in range(U - AHEAD, U):
                scatter_3((0, NG - 3), k)
            for g in (NG - 2, NG - 1):
                ready_3((0, g))
                for k in range(U):
                    scatter_3((0, g), k)
            for s in c_sc:
                pool.wait_ge(s, 16 * NT // 2)

            def add_4(b):
                h = b[1] % 2
                pool.wait_ge(z_ld[h], slot_count(b, 32))
                wait(pool, z_y, count(b, 1, -1))
                pool.tensor_tensor(pre[h][:, :], ld_a[h][:, :], ld_b[h][:, :], ALU.add).then_inc(z_sum, 1)

            def norm_4(b):
                h = b[1] % 2
                pool.wait_ge(z_r, count(b, 1, 1))
                wait(pool, z_st[h], slot_count(b, 16) - 16)
                pool.tensor_tensor(nodes(ysq[h][:, :]), rows(b), small(rsd, b).unsqueeze(2).broadcast_to([P, BW * J, D]),
                                   ALU.mult).then_inc(z_out, 1)

            staged(pool, [add_4] + [None] * 5 + [norm_4], NB)

        @block.scalar
        def _(act):
            act.wait_ge(s_sum, 1)
            act.activation(rnorm[:, :], rsum[:, :], ACT.Sqrt).then_inc(s_norm, 1)
            act.wait_ge(s_wld, N_WLD)

            def copy_sums(c, sem_):
                blocks = psum[2 + c][:, :].rearrange("p (b q) -> p b q", q=P)
                even = (U + 1) // 2
                act_copy(act, msg_t[:, c, 0:even, :], blocks[0:D, 0:even, :]).then_inc(sem_, 1)
                act_copy(act, msg_t[:, c, even:U, :], blocks[D:2 * D, 0:U - even, :]).then_inc(sem_, 1)

            def step_a(g):
                act.wait_ge(a_msg_p, count(g, 1, 1))
                wait(act, a_pay_p, count(g, 1))
                copy_sums(0, a_msg)
                act.wait_ge(a_pay_p, count(g, 1, 1))
                act_copy(act, pay_in[:, bass.ds(count(g, U), U), :],
                         psum[6][:, 0:U * D].rearrange("p (t f) -> p t f", t=U)).then_inc(a_pay, 1)

            def step_b(g):
                h = g[1] % 2
                act.wait_ge(b_xt_p, count(g, 1, 1))
                wait(act, b_xw1_p, count(g, 1))
                act_copy(act, xt[:, 0:4, :], psum[0][:, :]).then_inc(b_xt, 1)
                act_copy(act, xt[:, 4:U, :], psum[1][:, 0:3 * P]).then_inc(b_xt, 1)
                act.wait_ge(b_xw1_p, count(g, 1, 1))
                w0 = count(g, U)
                act_copy(act, res[:, bass.ds(w0, 4), :], psum[4][:, :].rearrange("p (w c) -> p w c", w=4)).then_inc(b_xw1, 1)
                act_copy(act, res[:, bass.ds(w0 + 4, 3), :], psum[5][:, 0:3 * P].rearrange("p (w c) -> p w c", w=3)).then_inc(b_xw1, 1)
                act.wait_ge(b_msg_p, count(g, 1, 1))
                wait(act, b_pay_p, count(g, 1))
                copy_sums(1, b_msg)
                for s in b_sc:
                    wait(act, s, count(g, 16 * U, -16 * U))
                act.wait_ge(a_pay, count(g, 1, 1))
                act_copy(act, pay[h][:, 0], pay_in[:, bass.ds(w0, U), :])
                act.wait_ge(b_pay_p, count(g, 1, 1))
                act_copy(act, pay[h][:, 1], psum[7][:, 0:U * D].rearrange("p (t f) -> p t f", t=U)).then_inc(b_pay, 1)

            led(act, step_a, step_b)

            def tanh(n, b):
                h = b[1] % 2
                act.wait_ge(m_mm[n], count(b, 1, 1))
                wait(act, m_mm[n + 1], count(b, 1, -1))
                act.activation(hid[n][h][:, :], bank_2[n][h][:, :], ACT.Tanh, bias=bias[:, n:n + 1]).then_inc(m_act[n], 1)

            def square_2(b):
                h = b[1] % 2
                act.wait_ge(m_y, count(b, 1, 1))
                wait(act, m_ssq, count(b, 1, -1))
                act.activation(wins(ysq[h][:, :]), batch(b), ACT.Square, scale=D ** -0.5).then_inc(m_sq, 1)

            staged(act, [lambda b, n=n: tanh(n, b) for n in range(4)] + [None, None, square_2], NB)

            def hidden_3(g):
                h = g[1] % 2
                act.wait_ge(c_arow[h], slot_count(g, 16))
                wait(act, c_r, count(g, U, -U))
                act.activation(ht[h][0:HID, :], arow[h][:, :], ACT.Relu, bias=rw1c[:, 1:2], scale=rw1c[:, 0:1]).then_inc(c_ht, 1)

            def features_3(g):
                h = g[1] % 2
                act.wait_ge(c_gat[h], slot_count(g, 16 * U))
                wait(act, c_fk, count(g, 1))
                vec = gat[h][:, :, 8:32].rearrange("p t (v i) -> p t v i", i=3)
                act_copy(act, feat5[:, :, :, 0:3], vec)
                act_copy(act, feat5[:, :, :, 3:5], vec[:, :, :, 0:2])
                wait(act, c_use, count(g, U, -U))
                act_copy(act, fd[h][:, :, 0, :], gat[h][:, :, 0:8])
                for i in range(3):
                    last = act_copy(act, fk[h][:, :, i, 0, :], vec[:, :, :, i])
                last.then_inc(c_feat, 1)

            def copy_3(g):
                h = g[1] % 2
                act.wait_ge(c_pay_p, count(g, 1, 1))
                for c in range(2):
                    wait(act, c_sc[c], landed_3((g[0], g[1] - 2), c))
                act_copy(act, pay1[h][:, :, :], psum[7][:, 0:U * D].rearrange("p (t f) -> p t f", t=U)).then_inc(c_pay, 1)

            def step_3(g, first=False):
                hidden_3(g)
                features_3(g)
                if not first:
                    copy_3((g[0], g[1] - 1))

            step_3((0, 0), first=True)
            step_3((0, 1))
            with act.Fori(0, NG // 2 - 1) as i:
                step_3((i, 2))
                step_3((i, 3))
            copy_3((0, NG - 1))

            def square_4(b):
                h = b[1] % 2
                act.wait_ge(z_y, count(b, 1, 1))
                wait(act, z_var, count(b, 1, -1))
                act.activation(wins(ld_c[h][:, :]), batch(b), ACT.Square, scale=D ** -0.5).then_inc(z_sq, 1)

            def root_4(b):
                act.wait_ge(z_var, count(b, 1, 1))
                act.activation(small(dev, b), small(var, b), ACT.Sqrt, bias=eps[:, :]).then_inc(z_root, 1)

            staged(act, [square_4, None, root_4], NB)

        @block.tensor
        def _(pe):
            pe.wait_ge(s_const, 5)
            pe.wait_ge(s_erow, 1)
            for n in range(6):
                for c in range(2):
                    col = (n % 2) * NT + c * HALF
                    ins = pe.transpose(psum[n // 2][:, col:col + HALF], val_rows[:, n, c, :], ident[0:HALF, 0:HALF])
            ins.then_inc(s_ecol, 1)
            pe.wait_ge(s_ready, 1)
            pe.wait_ge(s_wld, N_WLD)

            def sums(c):
                for k in range(U):
                    r = D * (k % 2)
                    ins = pe.matmul(psum[2 + c][r:r + D, P * (k // 2):P * (k // 2) + P], wmsg[:, c, k, :], same[:, c, k, :],
                                    start=True, stop=True)
                return ins

            def projections(c):
                for k in range(U):
                    ins = pe.matmul(psum[6 + c][:, D * k:D * k + D], msg_t[:, c, (k % 2) * ((U + 1) // 2) + k // 2, :], w1ab[:, c, :],
                                    start=True, stop=True)
                return ins

            def step_a(g):
                pe.wait_ge(a_same, count(g, 1, 1))
                pe.wait_ge(a_wmsg, count(g, 1, 1))
                wait(pe, a_msg, count(g, 2))
                sums(0).then_inc(a_msg_p, 1)
                pe.wait_ge(a_msg, count(g, 2, 2))
                wait(pe, a_pay, count(g, 1))
                projections(0).then_inc(a_pay_p, 1)

            def step_b(g):
                h = g[1] % 2
                pe.wait_ge(b_xw[h], slot_count(g, 16))
                wait(pe, b_xt, count(g, 2))
                for k in range(U):
                    ins = pe.transpose(two_banks(0)(k), xw[h][:, k, :], ident[:, :])
                ins.then_inc(b_xt_p, 1)
                pe.wait_ge(b_xt, count(g, 2, 2))
                wait(pe, b_xw1, count(g, 2))
                for k in range(U):
                    ins = pe.matmul(two_banks(4)(k), xt[:, k, :], w1c[:, :], start=True, stop=True)
                ins.then_inc(b_xw1_p, 1)
                pe.wait_ge(b_same, count(g, 1, 1))
                pe.wait_ge(b_wmsg, count(g, 1, 1))
                wait(pe, b_msg, count(g, 2))
                sums(1).then_inc(b_msg_p, 1)
                pe.wait_ge(b_msg, count(g, 2, 2))
                wait(pe, b_pay, count(g, 1))
                projections(1).then_inc(b_pay_p, 1)

            led(pe, step_a, step_b)
            pe.wait_ge(b_xw1, 2 * NG)
            pe.wait_ge(b_pay, NG)
            for s in (a_msg, b_msg):
                pe.wait_ge(s, 2 * NG)
            pe.wait_ge(a_pay, NG)

            def turn(b):
                h = b[1] % 2
                pe.wait_ge(m_pre, count(b, 1, 1))
                wait(pe, m_act[0], count(b, 1, held_2[0]))
                for w in range(BW):
                    ins = pe.transpose(bank_2[0][h][:, P * w:P * w + P], pre[h][:, P * w:P * w + P], ident[:, :])
                ins.then_inc(m_mm[0], 1)

            def layer(n, b):
                h = b[1] % 2
                pe.wait_ge(m_act[n - 1], count(b, 1, 1))
                wait(pe, m_act[n], count(b, 1, held_2[n]))
                pe.matmul(bank_2[n][h][:, :], wl[n - 1][:, :], hid[n - 1][h][:, :], start=True, stop=True).then_inc(m_mm[n], 1)

            def back(b):
                h = b[1] % 2
                pe.wait_ge(m_act[3], count(b, 1, 1))
                wait(pe, m_y, count(b, 1, held_2[4]))
                for w in range(BW):
                    ins = pe.matmul(bank_2[4][h][:, P * w:P * w + P], hid[3][h][:, P * w:P * w + P], centre[:, :],
                                    start=True, stop=True)
                ins.then_inc(m_mm[4], 1)

            staged(pe, [turn] + [lambda b, n=n: layer(n, b) for n in range(1, 4)] + [back], NB)
            pe.wait_ge(s_wprep, 1)
            for s in m_act:
                pe.wait_ge(s, NB)
            pe.wait_ge(m_y, NB)
            pe.wait_ge(c_ones, 2)

            def radial(g, k):
                h = g[1] % 2
                if k == 0:
                    pe.wait_ge(c_ht, count(g, 1, 1))
                wait(pe, c_use, count(g, U, k + 1 - U))
                pe.matmul(psum[k][:, 0:RC], ht[h][:, P * k:P * k + P], rw[:, :, :].rearrange("p a b -> p (a b)"),
                          start=True, stop=True).then_inc(c_r, 1)

            def sum_3(g):
                h = g[1] % 2
                pe.wait_ge(c_same, count(g, 1, 1))
                pe.wait_ge(c_msg, count(g, 1, 1))
                wait(pe, c_pay, count(g, 1))
                for k in range(U):
                    ins = pe.matmul(psum[7][:, D * k:D * k + D], same[:, h, k, :], msg1[h][:, k, :], start=True, stop=True)
                ins.then_inc(c_pay_p, 1)

            def step_3(g, first=False):
                for k in range(U):
                    radial(g, k)
                    if k == 2 and not first:
                        sum_3((g[0], g[1] - 1))

            step_3((0, 0), first=True)
            step_3((0, 1))
            with pe.Fori(0, NG // 2 - 1) as i:
                step_3((i, 2))
                step_3((i, 3))
            sum_3((0, NG - 1))

        @block.vector
        def _(dve):
            dve.memset(zeros[:, :], 0.0).then_inc(s_fill, 1)
            for t in (w1c, *wl):
                dve.memset(t[:, :], 0.0).then_inc(s_fill, 1)
            dve.memset(centre[:, :], 0.0).then_inc(s_fill, 1)
            dve.memset(key_i[:, :, NT:NT + 2 * U], 0).then_inc(s_fill, 1)
            dve.memset(eps[:, :], EPS)
            dve.memset(sdst_all[:, NT:NT + U], 0).then_inc(s_fill, 1)
            dve.wait_ge(s_fill, 8)
            for j in range(J):
                s = slice(D * j, D * j + D)
                dve.memset(centre[s, s], -1.0 / D).then_inc(s_fill, 1)
            dve.wait_ge(s_fill, 12)
            dve.wait_ge(s_const, 5)
            dve.tensor_tensor(centred[:, :], centre[:, :], ident[:, :], ALU.add).then_inc(s_fill, 1)
            dve.wait_ge(s_fill, 13)
            dve.tensor_copy(centre[:, :], centred[:, :]).then_inc(s_fill, 1)
            dve.tensor_copy(tr_f[:, :], tr_i[:, :]).then_inc(s_fill, 1)

            dve.wait_ge(s_eld, 64)
            dve.tensor_copy(val_rows[:, 0:2], idx_rows[:, :, :, :])
            e3 = ea_rows[:, :, :].rearrange("r c (q i) -> r c q i", i=3)
            for n, i in enumerate((1, 2, 0)):
                ins = dve.tensor_copy(val_rows[:, 3 + n], e3[:, :, :, i])
            ins.then_inc(s_erow, 1)
            dve.wait_ge(s_ecol, 1)
            prep = Chain(dve, s_prep, 10)
            prep.begin((0, 0))
            keys = psum[0][:, 0:2 * NT].rearrange("p (c t) -> p c t", c=2)
            prep.mark(dve.tensor_copy(key_i[:, :, 0:NT], keys))
            prep.need()
            for h in range(2):
                dve.tensor_copy(gidx[h][:, :], key_i[:, 0, U * h:U * h + U]).then_inc(a_idx, 1)
            for h in range(2):
                dve.tensor_copy(gidx_b[h][:, :], key_i[:, 1, U * h:U * h + U]).then_inc(b_idx, 1)
            prep.mark(dve.tensor_copy(key_f[:, :, :], keys))
            dve.wait_ge(s_fill, 15)
            prep.mark(dve.tensor_scalar(to_spare[:, :, :], keys, -1.0, tr_f[:, :], ALU.mult, ALU.add))
            prep.mark(dve.tensor_copy(w1e[:, :], psum[1][:, 0:NT]))
            prep.mark(dve.tensor_copy(rel[:, :, 0], psum[1][:, NT:2 * NT]))
            prep.mark(dve.tensor_copy(rel[:, :, 1:3], psum[2][:, 0:2 * NT].rearrange("p (c t) -> p t c", c=2)))
            prep.need()
            prep.mark(dve.tensor_tensor(relsq[:, :, :], rel[:, :, :], rel[:, :, :], ALU.mult))
            prep.need()
            dve.tensor_reduce(rsum[:, :], relsq[:, :, :], AX_X, ALU.add).then_inc(s_sum, 1)
            dve.wait_ge(s_norm, 1)
            prep.mark(dve.reciprocal(rinv[:, :], rnorm[:, :]))
            prep.need()
            prep.mark(dve.tensor_tensor(dir5[:, :, 0:3], rel[:, :, :], rinv[:, :].unsqueeze(2).broadcast_to([P, NT, 3]), ALU.mult))
            prep.need()
            prep.mark(dve.tensor_copy(dir5[:, :, 3:5], dir5[:, :, 0:2]))
            prep.end()
            prep.need()
            dve.wait_ge(b_idx, 2)
            dve.memset(row_f[:, :, :], 0.0).then_inc(s_ready, 1)

            def targets(ch, g, c, rows, sem_same):
                h = g[1] % 2
                key = 1 - c
                ts = bass.ds(count(g, U), U)
                dve.tensor_tensor(same[:, c], rows[h][:, :, :], key_f[:, key, ts].unsqueeze(2).broadcast_to([P, U, P]),
                                  ALU.is_equal).then_inc(sem_same, 1)
                dve.wait_ge(sem_same, count(g, 1, 1))
                ch.mark(dve.tensor_tensor(earlier[:, :, :], same[:, c], lower[:, :].unsqueeze(1).broadcast_to([P, U, P]), ALU.mult))
                ch.need()
                ch.mark(dve.tensor_reduce(dups[:, c, :], earlier[:, :, :], AX_X, ALU.add))
                ch.need()
                ch.mark(dve.scalar_tensor_tensor(out=spare_step[:, c, :], in0=dups[:, c, :], scalar=1.0,
                                                 in1=to_spare[:, key, ts], op0=ALU.min, op1=ALU.mult))
                ch.need()
                ch.mark(dve.tensor_tensor(row_f[:, c, :], spare_step[:, c, :], key_f[:, key, ts], ALU.add))
                ch.need()

            def weigh(g, c, rows):
                return dve.tensor_tensor(wmsg[:, c], rows[:, :, :],
                                         w1e[:, bass.ds(count(g, U), U)].unsqueeze(2).broadcast_to([P, U, D]), ALU.mult)

            cha = Chain(dve, a_dve, 5)

            def step_a(g):
                h = g[1] % 2
                t0 = count(g, U)
                cha.begin(g)
                dve.wait_ge(a_rows[h], slot_count(g, 16))
                wait(dve, a_msg_p, count(g, 1))
                targets(cha, g, 0, rows_d, a_same)
                cha.mark(dve.tensor_copy(sdst_all[:, bass.ds(t0, U)], row_f[:, 0, :]))
                dve.wait_ge(a_gat[h], slot_count(g, 16 * U))
                dve.tensor_copy(gidx[h][:, :], key_i[:, 0, bass.ds(t0 + 2 * U, U)]).then_inc(a_idx, 1)
                weigh(g, 0, gat[h]).then_inc(a_wmsg, 1)
                cha.end()

            chb = Chain(dve, b_dve, 5)

            def step_b(g):
                h = g[1] % 2
                t0 = count(g, U)
                chb.begin(g)
                dve.wait_ge(b_rows[h], slot_count(g, 16))
                wait(dve, b_msg_p, count(g, 1))
                targets(chb, g, 1, rows_s, b_same)
                dve.wait_ge(b_gat[h], slot_count(g, 16 * U))
                dve.tensor_copy(gidx_b[h][:, :], key_i[:, 1, bass.ds(t0 + 2 * U, U)]).then_inc(b_idx, 1)
                weigh(g, 1, gat_b[h]).then_inc(b_wmsg, 1)
                for s in b_sc:
                    wait(dve, s, count(g, 16 * U, -16 * U))
                dve.wait_ge(a_dve, count(g, 5, 5))
                dve.tensor_copy(sidx[h][:, 0, :], sdst_all[:, bass.ds(t0, U)])
                dve.tensor_copy(sidx[h][:, 1, :], row_f[:, 1, :]).then_inc(b_sidx, 1)
                dve.wait_ge(b_xw[h], slot_count(g, 16))
                xn = xw[h][:, :, :].rearrange("p w (j f) -> p (w j) f", f=D)
                chb.mark(dve.tensor_reduce(xmean[:, :], xn, AX_X, ALU.add))
                chb.need()
                wait(dve, b_xst[h], slot_count(g, 16) - 16)
                dve.scalar_tensor_tensor(out=xcen[h][:, :, :].rearrange("p w (j f) -> p (w j) f", f=D),
                                         in0=xmean[:, :].unsqueeze(2).broadcast_to([P, U * J, D]), scalar=-1.0 / D, in1=xn,
                                         op0=ALU.mult, op1=ALU.add).then_inc(b_xcen, 1)
                chb.end()

            led(dve, step_a, step_b)

            dve.wait_ge(s_wld, N_WLD)
            b = [rw_raw[:, 64 * n:64 * n + 64].rearrange("p (u v) -> p u v", v=8) for n in range(3)]
            b11 = rw_raw[:, 192:384].rearrange("p (u v k) -> p u v k", v=8, k=3)
            dve.tensor_scalar(rw[:, 0:8, 0:8], b[0], C_00, None, ALU.mult)
            dve.tensor_scalar(rw[:, 0:8, 8:16], b[1], C_00, None, ALU.mult)
            dve.tensor_scalar(rw[:, 8:16, 0:8], b[2], C_10, None, ALU.mult)
            dve.tensor_scalar(rw[:, 8:16, 8:16], b11[:, :, :, 2], C_11_2, None, ALU.mult)
            dve.tensor_scalar(rw[:, 16:24, 8:16], b11[:, :, :, 1], C_11_1, None, ALU.mult)
            dve.tensor_scalar(rw_t[:, :, :], b11[:, :, :, 2], -C_11_2 / 3.0, None, ALU.mult).then_inc(s_wchain, 1)
            dve.wait_ge(s_wchain, 1)
            dve.scalar_tensor_tensor(out=rw[:, 16:24, 0:8], in0=b11[:, :, :, 0], scalar=C_11_0, in1=rw_t[:, :, :],
                                     op0=ALU.mult, op1=ALU.add).then_inc(s_wprep, 1)

            def add_2(b):
                h = b[1] % 2
                dve.wait_ge(m_mm[4], count(b, 1, 1))
                dve.wait_ge(m_xc[h], slot_count(b, 16))
                dve.tensor_tensor(batch(b), wins(bank_2[4][h][:, :]), wins(ld_c[h][:, :]), ALU.add).then_inc(m_y, 1)

            def squares_2(b):
                h = b[1] % 2
                dve.wait_ge(m_sq, count(b, 1, 1))
                dve.tensor_reduce(ssq_2[:, h, :], nodes(ysq[h][:, :]), AX_X, ALU.add).then_inc(m_ssq, 1)

            mch = Chain(dve, m_dve, 11, two_steps=True)

            def root_2(b):
                last = b[1] == NB - 1
                if b[1] % 2 == 0 and not last:
                    return
                mch.begin(b)
                dve.wait_ge(m_ssq, count(b, 1, 1))
                n = BW * J if last else 2 * BW * J
                v, y, t = vps[:, 0:n], newton[0][:, 0:n], newton[1][:, 0:n]
                mch.mark(dve.tensor_scalar(v, ssq_2[:, :, :].rearrange("p b n -> p (b n)")[:, 0:n], EPS, None, ALU.add))
                mch.need()
                mch.mark(dve.tensor_scalar(y.bitcast(I32), v.bitcast(I32), -0.5, float(0x5f3759df), ALU.mult, ALU.add))
                for _ in range(3):
                    mch.need()
                    mch.mark(dve.tensor_tensor(t, y, y, ALU.mult))
                    mch.need()
                    mch.mark(dve.scalar_tensor_tensor(out=t, in0=t, scalar=-0.5, in1=v, op0=ALU.mult, op1=ALU.mult))
                    mch.need()
                    mch.mark(dve.scalar_tensor_tensor(out=y, in0=t, scalar=1.5, in1=y, op0=ALU.add, op1=ALU.mult))
                mch.need()
                for m, a in enumerate((b,) if last else ((b[0], b[1] - 1), b)):
                    root = newton[0][:, BW * J * m:BW * J * (m + 1)]
                    dve.tensor_tensor(rows(a), rows(a), root.unsqueeze(2).broadcast_to([P, BW * J, D]), ALU.mult).then_inc(m_x1, 1)
                mch.end()

            def norm_2(b):
                squares_2(b)
                root_2(b)

            staged(dve, [None, None, norm_2], NB, head=add_2)

            for h in range(2):
                dve.memset(ht[h][HID:HID + 1, :], 1.0).then_inc(c_ones, 1)
            for h in range(2):
                dve.tensor_copy(gidx[h][:, :], key_i[:, 0, U * h:U * h + U]).then_inc(c_gidx, 1)
            cch = Chain(dve, c_dve, 2)

            def reduce_3(g, k):
                q = k % 3
                dve.wait_ge(c_use, count(g, U, k + 1))
                dve.tensor_reduce(red_s[:, k, :], prod_s[q][:, :, :], AX_X, ALU.add)
                dve.tensor_reduce(red_v[:, k, :, :], prod_v[q][:, :, :, :], AX_X, ALU.add).then_inc(c_red, 1)

            def step_3(g):
                h = g[1] % 2
                t0 = count(g, U)
                ts = bass.ds(t0, U)
                cch.begin(g)
                dve.wait_ge(c_rows[h], slot_count(g, 16))
                wait(dve, c_pay_p, count(g, 1, -1))
                dve.tensor_tensor(same[:, h], rows_d[h][:, :, :], key_f[:, 1, ts].unsqueeze(2).broadcast_to([P, U, P]),
                                  ALU.is_equal).then_inc(c_same, 1)
                dve.wait_ge(c_feat, count(g, 1, 1))
                dve.tensor_copy(gidx[h][:, :], key_i[:, 0, bass.ds(t0 + 2 * U, U)]).then_inc(c_gidx, 1)

                def along(a):
                    return dir5[:, ts, a:a + 3].unsqueeze(2).broadcast_to([P, U, 8, 3])

                dve.tensor_tensor(dprod[:, :, :, :], feat5[:, :, :, 0:3], along(0), ALU.mult)
                dve.tensor_tensor(kp[:, 0], feat5[:, :, :, 2:5], along(1), ALU.mult)
                cch.mark(dve.tensor_tensor(kp[:, 1], feat5[:, :, :, 1:4], along(2), ALU.mult))
                cch.need()
                dve.tensor_reduce(fd[h][:, :, 1, :], dprod[:, :, :, :], AX_X, ALU.add)
                dve.tensor_tensor(fk[h][:, :, :, 1, :].rearrange("p t i v -> p t v i"), kp[:, 0], kp[:, 1],
                                  ALU.subtract).then_inc(c_fk, 1)
                dve.wait_ge(c_fk, count(g, 1, 1))
                for k in range(U):
                    q = k % 3
                    dve.wait_ge(c_r, count(g, U, k + 1))
                    wait(dve, c_red, count(g, U, max(k - 2, 0)))
                    r_s = psum[k][:, 0:256].rearrange("p (u v) -> p u v", v=16)
                    r_v = psum[k][:, 256:384].rearrange("p (u v) -> p u v", v=16)
                    dve.tensor_tensor(prod_s[q][:, :, :], r_s, fd[h][:, k].rearrange("p a v -> p (a v)").unsqueeze(1).broadcast_to([P, 16, 16]),
                                      ALU.mult)
                    dve.tensor_tensor(prod_v[q][:, :, :, :], r_v.unsqueeze(2).broadcast_to([P, 8, 3, 16]),
                                      fk[h][:, k].rearrange("p i a v -> p i (a v)").unsqueeze(1).broadcast_to([P, 8, 3, 16]),
                                      ALU.mult).then_inc(c_use, 1)
                    if k >= 1:
                        reduce_3(g, k - 1)
                reduce_3(g, U - 1)
                dve.wait_ge(c_red, count(g, U, U))
                cch.mark(dve.tensor_tensor(rq[:, :, :, :], red_s[:, :, 8:16].unsqueeze(3).broadcast_to([P, U, 8, 3]), along(0), ALU.mult))
                cch.need()
                dve.tensor_copy(msg1[h][:, :, 0:8], red_s[:, :, 0:8])
                dve.tensor_tensor(msg1[h][:, :, 8:32].rearrange("p t (u i) -> p t u i", i=3), rq[:, :, :, :], red_v[:, :, :, :],
                                  ALU.add).then_inc(c_msg, 1)
                for c in range(2):
                    wait(dve, c_sc[c], landed_3((g[0], g[1] - 2), c))
                dve.tensor_copy(sidx[h][:, 0, :], sdst_all[:, ts]).then_inc(c_sidx, 1)
                cch.end()

            over_pairs(dve, step_3, NG)

            def sum_4(b):
                h = b[1] % 2
                dve.wait_ge(z_sum, count(b, 1, 1))
                wait(dve, z_y, count(b, 1))
                dve.tensor_reduce(ssq[:, :], nodes(pre[h][:, :]), AX_X, ALU.add).then_inc(z_n, 1)

            def centre_4(b):
                h = b[1] % 2
                dve.wait_ge(z_n, count(b, 1, 1))
                dve.scalar_tensor_tensor(out=rows(b), in0=ssq[:, :].unsqueeze(2).broadcast_to([P, BW * J, D]),
                                         scalar=-1.0 / D, in1=nodes(pre[h][:, :]), op0=ALU.mult, op1=ALU.add).then_inc(z_y, 1)

            def var_4(b):
                h = b[1] % 2
                dve.wait_ge(z_sq, count(b, 1, 1))
                dve.tensor_reduce(small(var, b), nodes(ld_c[h][:, :]), AX_X, ALU.add).then_inc(z_var, 1)

            def inverse_4(b):
                dve.wait_ge(z_root, count(b, 1, 1))
                dve.reciprocal(small(rsd, b), small(dev, b)).then_inc(z_r, 1)

            staged(dve, [centre_4, None, var_4, None, inverse_4], NB, head=sum_4)


_INS = ["x", "src", "dst", "edge_attr_3", "edge_weight", "edge_weight1",
        "L0_gnn_W1", "L0_gnn_b1", "L0_gnn_W2", "L0_gnn_b2", "L0_gnn_W3", "L0_gnn_b3", "L0_gnn_W4", "L0_gnn_b4",
        "L1_gnn_w1", "L1_gnn_b1", "L1_gnn_w2", "L1_gnn_b2"]


def kernel(**inputs):
    import numpy as np
    import concourse.bacc as bacc
    from concourse.bass_utils import run_bass_kernel_spmd

    a = {n: np.asarray(inputs[n]) for n in _INS}
    more = NT * P - E
    a["x"] = np.concatenate([a["x"], np.zeros((NPAD - N, D), a["x"].dtype)])
    spare = np.arange(PAD_NODE, PAD_NODE + more)
    for n in ("src", "dst"):
        a[n] = np.concatenate([a[n], spare.astype(a[n].dtype)]).reshape(NT, P)
    a["edge_attr_3"] = np.concatenate([a["edge_attr_3"], np.ones((more, 3), a["edge_attr_3"].dtype)]).reshape(NT, P * 3)
    for n in ("edge_weight", "edge_weight1"):
        v = a[n].reshape(-1)
        a[n] = np.concatenate([v, np.zeros(more, v.dtype)]).reshape(NT, P)
    for n in ("L0_gnn_b1", "L0_gnn_b2", "L0_gnn_b3", "L0_gnn_b4", "L1_gnn_b1"):
        a[n] = a[n].reshape(-1, 1)
    a["L1_gnn_w1"] = a["L1_gnn_w1"].reshape(-1, 1)
    a["L1_gnn_b2"] = a["L1_gnn_b2"].reshape(1, -1)

    nc = bacc.Bacc("TRN2", target_bir_lowering=False, num_devices=1)
    arrays, args = {}, []
    for n in _INS:
        v = np.ascontiguousarray(a[n])
        arrays[f"in_{n}"] = v
        args.append(nc.dram_tensor(f"in_{n}", v.shape, mybir.dt.from_np(v.dtype), kind="ExternalInput").ap())
    out = nc.dram_tensor("out", (NPAD, D), F32, kind="ExternalOutput").ap()
    gnn_kernel(nc, *args, out)
    r = run_bass_kernel_spmd(nc, [arrays], core_ids=[0])
    return r.results[0]["out"][:N]
```
